# Optimizing a Trainium2 kernel written in Bass

```python
import numpy as np
import jax
import jax.numpy as jnp

def _softmax(x, axis=-1):
    return jax.nn.softmax(x, axis=axis)

def _gelu(x):
    return jax.nn.gelu(x, approximate=True)

def _silu(x):
    return jax.nn.silu(x)

def _sigmoid(x):
    return jax.nn.sigmoid(x)

def _layernorm(x, axis=-1, eps=1e-05):
    m = jnp.mean(x, axis=axis, keepdims=True)
    v = jnp.var(x, axis=axis, keepdims=True)
    return (x - m) / jnp.sqrt(v + eps)

def _scatter_add(tgt, idx, src, axis=0):
    return tgt.at[idx].add(src)

def _segment_sum(src, seg, n):
    return jax.ops.segment_sum(src, seg, n)
kernel_name = 'mk_decoder_postln_d2_seqx_r8_bf7d46'

def setup_inputs(seed: int=0):
    np.random.seed(seed)
    _w = jnp.asarray

    def _rec_inputs():
        import jax
        import jax.numpy as jnp
        _rk = jax.random.key(seed)
        x = -0.0002928 + 1 * jax.random.normal(jax.random.fold_in(_rk, 1), (32, 128, 128), jnp.float32)
        _lenS = 128 - jax.random.randint(jax.random.fold_in(_rk, 7), (32,), 0, max(1, 128 // 4) + 1, jnp.int32)
        _lenS2 = 128 - jax.random.randint(jax.random.fold_in(_rk, 8), (32,), 0, max(1, 128 // 4) + 1, jnp.int32)
        _ctx_1024P = jax.random.normal(jax.random.fold_in(_rk, 11), (32, 16, 128), jnp.float32)
        _ctx_1024c = jax.random.dirichlet(jax.random.fold_in(_rk, 511), 0.3 * jnp.ones((16,), jnp.float32), (32, 128))
        _ctx_1024t = jnp.einsum('bsk,bkd->bsd', _ctx_1024c, _ctx_1024P)
        _ctx_1024t = _ctx_1024t * jax.lax.rsqrt(jnp.mean(jnp.square(_ctx_1024t)) + 1e-12) * 0.953939
        ctx_1024 = -1.39393e-06 + 0.999914 * (_ctx_1024t + 0.3 * jax.random.normal(jax.random.fold_in(_rk, 611), (32, 128, 128), jnp.float32))
        fside_BxSx4_0 = jax.random.uniform(jax.random.fold_in(_rk, 12), (32, 128, 4), jnp.float32, 0.0, 0.999884)
        return (x, ctx_1024, fside_BxSx4_0)
    x, ctx_1024, fside_BxSx4_0 = _rec_inputs()

    def _L0_attn_setup():
        import jax, jax.numpy as jnp
        import numpy as np
        DIM, H, G = (128, 16, 4)
        HD = DIM // H
        HKV = H // G

        def rotate_half(x):
            return jnp.concatenate([-x[..., 1::2], x[..., ::2]], axis=-1)

        def rope_tables(seq_len, dim, dtype):
            inv_freq = 1.0 / 10000.0 ** (jnp.arange(0, dim, 2, dtype=jnp.float32) / dim)
            pos = jnp.arange(seq_len, dtype=jnp.float32)
            sinusoid = pos[:, None] * inv_freq[None, :]
            sin = jnp.concatenate([jnp.sin(sinusoid)] * 2, -1)
            cos = jnp.concatenate([jnp.cos(sinusoid)] * 2, -1)
            return (sin.astype(dtype)[None, :, None, :], cos.astype(dtype)[None, :, None, :])
        key = jax.random.key(seed)
        ks = jax.random.split(key, 9)
        s = 0.02
        return {'hidden_states': jax.random.normal(ks[0], (2, 256, DIM), jnp.float32), 'Wq': jax.random.normal(ks[1], (DIM, DIM), jnp.float32) * s, 'bq': jnp.zeros((DIM,), jnp.float32), 'Wk': jax.random.normal(ks[2], (DIM // G, DIM), jnp.float32) * s, 'bk': jnp.zeros((DIM // G,), jnp.float32), 'Wv': jax.random.normal(ks[3], (DIM // G, DIM), jnp.float32) * s, 'bv': jnp.zeros((DIM // G,), jnp.float32), 'Wo': jax.random.normal(ks[4], (DIM, DIM), jnp.float32) * s, 'bo': jnp.zeros((DIM,), jnp.float32)}
    _L0_attn_all = _L0_attn_setup()
    _L0_attn_in = {k: v for k, v in _L0_attn_all.items() if k in ('Wq', 'bq', 'Wk', 'bk', 'Wv', 'bv', 'Wo', 'bo')}
    del _L0_attn_all

    def _L0_xattn_setup():
        import jax, jax.numpy as jnp
        import numpy as np
        B, S, D = (1, 512, 128)
        NUM_HEADS, HEAD_DIM = (16, 64)
        WINDOW = 128
        EMBED = NUM_HEADS * HEAD_DIM
        key = jax.random.key(seed)
        ks = jax.random.split(key, 7)
        scale_in = 1.0 / np.sqrt(D)
        scale_e = 1.0 / np.sqrt(EMBED)
        return {'query': jax.random.normal(ks[0], (B, S, D), dtype=jnp.float32), 'key': jax.random.normal(ks[1], (B, S, D), dtype=jnp.float32), 'value': jax.random.normal(ks[2], (B, S, D), dtype=jnp.float32), 'Wq': jax.random.normal(ks[3], (D, EMBED), dtype=jnp.float32) * scale_in, 'Wk': jax.random.normal(ks[4], (D, EMBED), dtype=jnp.float32) * scale_in, 'Wv': jax.random.normal(ks[5], (D, EMBED), dtype=jnp.float32) * scale_in, 'Wo': jax.random.normal(ks[6], (EMBED, D), dtype=jnp.float32) * scale_e}
    _L0_xattn_all = _L0_xattn_setup()
    _L0_xattn_in = {k: v for k, v in _L0_xattn_all.items() if k in ('Wq', 'Wk', 'Wv', 'Wo')}
    del _L0_xattn_all

    def _L0_ffn_setup():
        import jax, jax.numpy as jnp
        import numpy as np
        B, S, D = (4, 256, 128)
        E, F = (8, 512)
        key = jax.random.key(seed)
        ks = jax.random.split(key, 5)
        x = jax.random.normal(ks[0], (B, S, D), dtype=jnp.float32)
        switch_w = jax.random.normal(ks[1], (D, E), dtype=jnp.float32) * D ** (-0.5)
        switch_b = jnp.zeros((E,), dtype=jnp.float32)
        w1 = jax.random.normal(ks[2], (E, D, F), dtype=jnp.float32) * D ** (-0.5)
        b1 = jnp.zeros((E, F), dtype=jnp.float32)
        w2 = jax.random.normal(ks[3], (E, F, D), dtype=jnp.float32) * F ** (-0.5)
        b2 = jnp.zeros((E, D), dtype=jnp.float32)
        return {'x': x, 'switch_w': switch_w, 'switch_b': switch_b, 'w1': w1, 'b1': b1, 'w2': w2, 'b2': b2}
    _L0_ffn_all = _L0_ffn_setup()
    _L0_ffn_in = {k: v for k, v in _L0_ffn_all.items() if k in ('switch_w', 'switch_b', 'w1', 'b1', 'w2', 'b2')}
    del _L0_ffn_all

    def _L1_attn_setup():
        import jax, jax.numpy as jnp
        import numpy as np
        from math import log2, ceil
        HEADS, DIM_HEAD, BLOCK, EPS = (16, 64, 16, 1e-08)
        key = jax.random.key(seed)
        k1, k2, k3, k4 = jax.random.split(key, 4)
        b, n, dim = (4, 512, 128)
        inner = HEADS * DIM_HEAD
        return {'x': jax.random.normal(k1, (b, n, dim), jnp.float32), 'w_qkv': jax.random.normal(k2, (inner * 3, dim), jnp.float32) * 0.02, 'w_out': jax.random.normal(k3, (dim, inner), jnp.float32) * 0.02, 'b_out': jax.random.normal(k4, (dim,), jnp.float32) * 0.02}
    _L1_attn_all = _L1_attn_setup()
    _L1_attn_in = {k: v for k, v in _L1_attn_all.items() if k in ('w_qkv', 'w_out', 'b_out')}
    del _L1_attn_all

    def _L1_xattn_setup():
        import jax, jax.numpy as jnp
        import numpy as np
        D_MODEL = 128
        H = 16
        D_K = 64
        D_V = 64
        D_G = D_MODEL // H
        WAVE_LEN = 1000.0
        B = 8
        N = 64

        def box_relational_embedding(boxes, dim_g=D_G):
            x_min, y_min, x_max, y_max = jnp.split(boxes, 4, axis=-1)
            cx = (x_min + x_max) * 0.5
            cy = (y_min + y_max) * 0.5
            w = x_max - x_min + 1.0
            h = y_max - y_min + 1.0
            delta_x = jnp.log(jnp.clip(jnp.abs((cx - jnp.swapaxes(cx, 1, 2)) / w), 0.001, None))
            delta_y = jnp.log(jnp.clip(jnp.abs((cy - jnp.swapaxes(cy, 1, 2)) / h), 0.001, None))
            delta_w = jnp.log(w / jnp.swapaxes(w, 1, 2))
            delta_h = jnp.log(h / jnp.swapaxes(h, 1, 2))
            pos = jnp.stack([delta_x, delta_y, delta_w, delta_h], axis=-1)
            n_freq = dim_g // 8
            feat_range = jnp.arange(n_freq, dtype=jnp.float32)
            dim_mat = 1.0 / WAVE_LEN ** (feat_range / n_freq)
            mul = (100.0 * pos)[..., None] * dim_mat
            b, n = (pos.shape[0], pos.shape[1])
            mul = mul.reshape(b, n, n, 4 * n_freq)
            return jnp.concatenate([jnp.sin(mul), jnp.cos(mul)], axis=-1)
        key = jax.random.key(seed)
        ks = jax.random.split(key, 12)
        s = 0.02
        inp = {'queries': jax.random.normal(ks[0], (B, N, D_MODEL), jnp.float32), 'keys': jax.random.normal(ks[1], (B, N, D_MODEL), jnp.float32), 'values': jax.random.normal(ks[2], (B, N, D_MODEL), jnp.float32), 'boxes': jax.random.uniform(ks[3], (B, N, 4), jnp.float32), 'Wq': jax.random.normal(ks[4], (H * D_K, D_MODEL), jnp.float32) * s, 'bq': jnp.zeros((H * D_K,), jnp.float32), 'Wk': jax.random.normal(ks[5], (H * D_K, D_MODEL), jnp.float32) * s, 'bk': jnp.zeros((H * D_K,), jnp.float32), 'Wv': jax.random.normal(ks[6], (H * D_V, D_MODEL), jnp.float32) * s, 'bv': jnp.zeros((H * D_V,), jnp.float32), 'Wo': jax.random.normal(ks[7], (D_MODEL, H * D_V), jnp.float32) * s, 'bo': jnp.zeros((D_MODEL,), jnp.float32), 'Wg': jax.random.normal(ks[8], (H, D_G), jnp.float32) * s, 'bg': jnp.zeros((H,), jnp.float32)}
        return inp
    _L1_xattn_all = _L1_xattn_setup()
    _L1_xattn_in = {k: v for k, v in _L1_xattn_all.items() if k in ('Wq', 'bq', 'Wk', 'bk', 'Wv', 'bv', 'Wo', 'bo', 'Wg', 'bg')}
    del _L1_xattn_all

    def _L1_ffn_setup():
        import jax, jax.numpy as jnp
        import numpy as np
        NEG_INF = -1e+30

        def _moe_forward(x, router_w, router_b, w1, b1, w2, b2, top_k=2):
            B, S, D = x.shape
            E = router_w.shape[1]
            logits = jnp.einsum('bsd,de->bse', x, router_w) + router_b
            top_vals, top_idx = jax.lax.top_k(logits, top_k)
            keep = jax.nn.one_hot(top_idx, E, dtype=logits.dtype).sum(-2) > 0
            sparse_logits = jnp.where(keep, logits, NEG_INF)
            gating = jax.nn.softmax(sparse_logits, axis=-1)
            xf = x.reshape(-1, D)
            gf = gating.reshape(-1, E)
            h = jax.nn.relu(jnp.einsum('td,edh->eth', xf, w1) + b1[:, None, :])
            y = jnp.einsum('eth,ehd->etd', h, w2) + b2[:, None, :]
            out = jnp.einsum('etd,te->td', y, gf)
            return out.reshape(B, S, D)
        key = jax.random.key(seed)
        ks = jax.random.split(key, 5)
        B, S, D, E, H = (2, 256, 128, 8, 512)
        scale = 0.02
        return {'x': jax.random.normal(ks[0], (B, S, D), dtype=jnp.float32), 'router_w': jax.random.normal(ks[1], (D, E), dtype=jnp.float32) * scale, 'router_b': jnp.zeros((E,), dtype=jnp.float32), 'w1': jax.random.normal(ks[2], (E, D, H), dtype=jnp.float32) * scale, 'b1': jnp.zeros((E, H), dtype=jnp.float32), 'w2': jax.random.normal(ks[3], (E, H, D), dtype=jnp.float32) * scale, 'b2': jnp.zeros((E, D), dtype=jnp.float32)}
    _L1_ffn_all = _L1_ffn_setup()
    _L1_ffn_in = {k: v for k, v in _L1_ffn_all.items() if k in ('router_w', 'router_b', 'w1', 'b1', 'w2', 'b2')}
    del _L1_ffn_all
    return {'x': x, 'ctx_1024': ctx_1024, 'fside_BxSx4_0': fside_BxSx4_0, 'L0_attn_Wq': _L0_attn_in['Wq'], 'L0_attn_bq': _L0_attn_in['bq'], 'L0_attn_Wk': _L0_attn_in['Wk'], 'L0_attn_bk': _L0_attn_in['bk'], 'L0_attn_Wv': _L0_attn_in['Wv'], 'L0_attn_bv': _L0_attn_in['bv'], 'L0_attn_Wo': _L0_attn_in['Wo'], 'L0_attn_bo': _L0_attn_in['bo'], 'L0_xattn_Wq': _L0_xattn_in['Wq'], 'L0_xattn_Wk': _L0_xattn_in['Wk'], 'L0_xattn_Wv': _L0_xattn_in['Wv'], 'L0_xattn_Wo': _L0_xattn_in['Wo'], 'L0_ffn_switch_w': _L0_ffn_in['switch_w'], 'L0_ffn_switch_b': _L0_ffn_in['switch_b'], 'L0_ffn_w1': _L0_ffn_in['w1'], 'L0_ffn_b1': _L0_ffn_in['b1'], 'L0_ffn_w2': _L0_ffn_in['w2'], 'L0_ffn_b2': _L0_ffn_in['b2'], 'L1_attn_w_qkv': _L1_attn_in['w_qkv'], 'L1_attn_w_out': _L1_attn_in['w_out'], 'L1_attn_b_out': _L1_attn_in['b_out'], 'L1_xattn_Wq': _L1_xattn_in['Wq'], 'L1_xattn_bq': _L1_xattn_in['bq'], 'L1_xattn_Wk': _L1_xattn_in['Wk'], 'L1_xattn_bk': _L1_xattn_in['bk'], 'L1_xattn_Wv': _L1_xattn_in['Wv'], 'L1_xattn_bv': _L1_xattn_in['bv'], 'L1_xattn_Wo': _L1_xattn_in['Wo'], 'L1_xattn_bo': _L1_xattn_in['bo'], 'L1_xattn_Wg': _L1_xattn_in['Wg'], 'L1_xattn_bg': _L1_xattn_in['bg'], 'L1_ffn_router_w': _L1_ffn_in['router_w'], 'L1_ffn_router_b': _L1_ffn_in['router_b'], 'L1_ffn_w1': _L1_ffn_in['w1'], 'L1_ffn_b1': _L1_ffn_in['b1'], 'L1_ffn_w2': _L1_ffn_in['w2'], 'L1_ffn_b2': _L1_ffn_in['b2']}

def reference(x, ctx_1024, fside_BxSx4_0, L0_attn_Wq, L0_attn_bq, L0_attn_Wk, L0_attn_bk, L0_attn_Wv, L0_attn_bv, L0_attn_Wo, L0_attn_bo, L0_xattn_Wq, L0_xattn_Wk, L0_xattn_Wv, L0_xattn_Wo, L0_ffn_switch_w, L0_ffn_switch_b, L0_ffn_w1, L0_ffn_b1, L0_ffn_w2, L0_ffn_b2, L1_attn_w_qkv, L1_attn_w_out, L1_attn_b_out, L1_xattn_Wq, L1_xattn_bq, L1_xattn_Wk, L1_xattn_bk, L1_xattn_Wv, L1_xattn_bv, L1_xattn_Wo, L1_xattn_bo, L1_xattn_Wg, L1_xattn_bg, L1_ffn_router_w, L1_ffn_router_b, L1_ffn_w1, L1_ffn_b1, L1_ffn_w2, L1_ffn_b2):
    import jax
    import jax.numpy as jnp

    def _L0_attn_ref(hidden_states, Wq, bq, Wk, bk, Wv, bv, Wo, bo):
        import jax, jax.numpy as jnp
        import numpy as np
        DIM, H, G = (128, 16, 4)
        HD = DIM // H
        HKV = H // G

        def rotate_half(x):
            return jnp.concatenate([-x[..., 1::2], x[..., ::2]], axis=-1)

        def rope_tables(seq_len, dim, dtype):
            inv_freq = 1.0 / 10000.0 ** (jnp.arange(0, dim, 2, dtype=jnp.float32) / dim)
            pos = jnp.arange(seq_len, dtype=jnp.float32)
            sinusoid = pos[:, None] * inv_freq[None, :]
            sin = jnp.concatenate([jnp.sin(sinusoid)] * 2, -1)
            cos = jnp.concatenate([jnp.cos(sinusoid)] * 2, -1)
            return (sin.astype(dtype)[None, :, None, :], cos.astype(dtype)[None, :, None, :])
        b, t, _ = hidden_states.shape
        q = (hidden_states @ Wq.T + bq).reshape(b, t, H, HD)
        k = (hidden_states @ Wk.T + bk).reshape(b, t, HKV, HD)
        v = (hidden_states @ Wv.T + bv).reshape(b, t, HKV, HD)
        sin, cos = rope_tables(t, HD, q.dtype)
        q = q * cos + rotate_half(q) * sin
        k = k * cos + rotate_half(k) * sin
        k = jnp.repeat(k, G, axis=2)
        v = jnp.repeat(v, G, axis=2)
        scale = 1.0 / jnp.sqrt(jnp.float32(HD)).astype(q.dtype)
        scores = jnp.einsum('bthd,bshd->btsh', q, k) * scale
        probs = jax.nn.softmax(scores, axis=2)
        context = jnp.einsum('btsh,bshd->bthd', probs, v).reshape(b, t, DIM)
        return context @ Wo.T + bo

    def _L0_xattn_ref(query, key, value, Wq, Wk, Wv, Wo):
        import jax, jax.numpy as jnp
        import numpy as np
        B, S, D = (1, 512, 128)
        NUM_HEADS, HEAD_DIM = (16, 64)
        WINDOW = 128
        EMBED = NUM_HEADS * HEAD_DIM
        Bq, Sq, _ = query.shape
        q = (query @ Wq).reshape(Bq, Sq, NUM_HEADS, HEAD_DIM).transpose(0, 2, 1, 3)
        k = (key @ Wk).reshape(Bq, Sq, NUM_HEADS, HEAD_DIM).transpose(0, 2, 1, 3)
        v = (value @ Wv).reshape(Bq, Sq, NUM_HEADS, HEAD_DIM).transpose(0, 2, 1, 3)
        idx = jnp.arange(Sq)
        local_mask = jnp.abs(idx[:, None] - idx[None, :]) > WINDOW
        scores = jnp.einsum('bhqd,bhkd->bhqk', q, k) / jnp.sqrt(jnp.float32(HEAD_DIM))
        scores = jnp.where(local_mask, -jnp.inf, scores)
        attn = jax.nn.softmax(scores, axis=-1)
        out = jnp.einsum('bhqk,bhkd->bhqd', attn, v)
        out = out.transpose(0, 2, 1, 3).reshape(Bq, Sq, EMBED)
        return out @ Wo

    def _L0_ffn_ref(x, switch_w, switch_b, w1, b1, w2, b2):
        import jax, jax.numpy as jnp
        import numpy as np
        B, S, D = (4, 256, 128)
        E, F = (8, 512)
        b, s, d = x.shape
        t = x.reshape(-1, d)
        logits = t @ switch_w + switch_b
        route_prob = jax.nn.softmax(logits, axis=-1)
        route_prob_max = jnp.max(route_prob, axis=-1)
        routes = jnp.argmax(route_prob, axis=-1)
        out = jnp.zeros_like(t)
        n_experts = w1.shape[0]
        for e in range(n_experts):
            h = jax.nn.gelu(t @ w1[e] + b1[e])
            y = h @ w2[e] + b2[e]
            mask = (routes == e)[:, None]
            out = jnp.where(mask, y, out)
        out = out * route_prob_max[:, None]
        return out.reshape(b, s, d)

    def _L1_attn_ref(x, w_qkv, w_out, b_out):
        import jax, jax.numpy as jnp
        import numpy as np
        from math import log2, ceil
        HEADS, DIM_HEAD, BLOCK, EPS = (16, 64, 16, 1e-08)
        b, n, dim = x.shape
        pad_to_len = 2 ** ceil(log2(n))
        if pad_to_len != n:
            x = jnp.pad(x, ((0, 0), (0, pad_to_len - n), (0, 0)))
        qkv = x @ w_qkv.T
        q, k, v = jnp.split(qkv, 3, axis=-1)

        def split_heads(t):
            return t.reshape(b, pad_to_len, HEADS, DIM_HEAD).transpose(0, 2, 1, 3).reshape(b * HEADS, pad_to_len, DIM_HEAD)
        q = split_heads(q) * DIM_HEAD ** (-0.5)
        k = split_heads(k)
        v = split_heads(v)
        num_levels = int(log2(pad_to_len // BLOCK)) - 1
        qkvs = [(q, k, v)]
        for _ in range(num_levels):
            q = q.reshape(q.shape[0], -1, 2, DIM_HEAD).mean(2)
            k = k.reshape(k.shape[0], -1, 2, DIM_HEAD).mean(2)
            v = v.reshape(v.shape[0], -1, 2, DIM_HEAD).sum(2)
            qkvs.append((q, k, v))
        neg_max = -jnp.finfo(x.dtype).max
        idx = jnp.arange(pad_to_len)
        Ysum = jnp.zeros((b * HEADS, pad_to_len, DIM_HEAD), x.dtype)
        Asum = jnp.zeros((b * HEADS, pad_to_len), x.dtype)
        for lvl, (ql, kl, vl) in enumerate(qkvs):
            B = ql.shape[0]
            nb = ql.shape[1] // BLOCK
            ql = ql.reshape(B, nb, BLOCK, DIM_HEAD)
            kl = kl.reshape(B, nb, BLOCK, DIM_HEAD)
            vl = vl.reshape(B, nb, BLOCK, DIM_HEAD)
            if lvl == 0:
                S = jnp.einsum('bnid,bnjd->bnij', ql, kl)
                S = jnp.where(jnp.triu(jnp.ones((BLOCK, BLOCK), bool), 1), neg_max, S)
                S = S - S.max(-1, keepdims=True)
                A = jnp.exp(S)
                y = jnp.einsum('bnij,bnjd->bnid', A, vl).reshape(B, pad_to_len, DIM_HEAD)
                Av = A.sum(-1).reshape(B, pad_to_len)
            else:
                q2 = ql.reshape(B, nb // 2, 2, BLOCK, DIM_HEAD)[:, :, 1]
                k1b = kl.reshape(B, nb // 2, 2, BLOCK, DIM_HEAD)[:, :, 0]
                v1b = vl.reshape(B, nb // 2, 2, BLOCK, DIM_HEAD)[:, :, 0]
                S = jnp.einsum('bnid,bnjd->bnij', q2, k1b)
                S = S - S.max(-1, keepdims=True)
                A = jnp.exp(S)
                y = jnp.einsum('bnij,bnjd->bnid', A, v1b)
                Av = A.sum(-1)
                y = jnp.pad(y[:, :, None], ((0, 0), (0, 0), (1, 0), (0, 0), (0, 0))).reshape(B, -1, DIM_HEAD)
                Av = jnp.pad(Av[:, :, None], ((0, 0), (0, 0), (1, 0), (0, 0))).reshape(B, -1)
                y = jnp.repeat(y, 2 ** lvl, axis=1)
                Av = jnp.repeat(Av, 2 ** lvl, axis=1)
            seq_key = (idx >> lvl << lvl) + (2 ** lvl - 1)
            keep = seq_key <= idx
            Ysum = Ysum + jnp.where(keep[None, :, None], y, 0.0)
            Asum = Asum + jnp.where(keep[None, :], Av, 0.0)
        out = Ysum / (Asum + EPS)[..., None]
        out = out.reshape(b, HEADS, pad_to_len, DIM_HEAD).transpose(0, 2, 1, 3).reshape(b, pad_to_len, HEADS * DIM_HEAD)
        out = out @ w_out.T + b_out
        return out[:, :n]

    def _L1_xattn_ref(queries, keys, values, boxes, Wq, bq, Wk, bk, Wv, bv, Wo, bo, Wg, bg):
        import jax, jax.numpy as jnp
        import numpy as np
        D_MODEL = 128
        H = 16
        D_K = 64
        D_V = 64
        D_G = D_MODEL // H
        WAVE_LEN = 1000.0
        B = 8
        N = 64

        def box_relational_embedding(boxes, dim_g=D_G):
            x_min, y_min, x_max, y_max = jnp.split(boxes, 4, axis=-1)
            cx = (x_min + x_max) * 0.5
            cy = (y_min + y_max) * 0.5
            w = x_max - x_min + 1.0
            h = y_max - y_min + 1.0
            delta_x = jnp.log(jnp.clip(jnp.abs((cx - jnp.swapaxes(cx, 1, 2)) / w), 0.001, None))
            delta_y = jnp.log(jnp.clip(jnp.abs((cy - jnp.swapaxes(cy, 1, 2)) / h), 0.001, None))
            delta_w = jnp.log(w / jnp.swapaxes(w, 1, 2))
            delta_h = jnp.log(h / jnp.swapaxes(h, 1, 2))
            pos = jnp.stack([delta_x, delta_y, delta_w, delta_h], axis=-1)
            n_freq = dim_g // 8
            feat_range = jnp.arange(n_freq, dtype=jnp.float32)
            dim_mat = 1.0 / WAVE_LEN ** (feat_range / n_freq)
            mul = (100.0 * pos)[..., None] * dim_mat
            b, n = (pos.shape[0], pos.shape[1])
            mul = mul.reshape(b, n, n, 4 * n_freq)
            return jnp.concatenate([jnp.sin(mul), jnp.cos(mul)], axis=-1)
        b, nq, _ = queries.shape
        nk = keys.shape[1]
        emb = box_relational_embedding(boxes)
        g = jax.nn.relu(jnp.einsum('bnmd,hd->bhnm', emb, Wg) + bg[None, :, None, None])
        q = (queries @ Wq.T + bq).reshape(b, nq, H, D_K).transpose(0, 2, 1, 3)
        k = (keys @ Wk.T + bk).reshape(b, nk, H, D_K).transpose(0, 2, 1, 3)
        v = (values @ Wv.T + bv).reshape(b, nk, H, D_V).transpose(0, 2, 1, 3)
        a = jnp.einsum('bhqd,bhkd->bhqk', q, k) / jnp.sqrt(jnp.float32(D_K))
        mn = jax.nn.softmax(jnp.log(jnp.clip(g, 1e-06, None)) + a, axis=-1)
        out = jnp.einsum('bhqk,bhkd->bqhd', mn, v).reshape(b, nq, H * D_V)
        return out @ Wo.T + bo

    def _L1_ffn_ref(x, router_w, router_b, w1, b1, w2, b2):
        import jax, jax.numpy as jnp
        import numpy as np
        NEG_INF = -1e+30

        def _moe_forward(x, router_w, router_b, w1, b1, w2, b2, top_k=2):
            B, S, D = x.shape
            E = router_w.shape[1]
            logits = jnp.einsum('bsd,de->bse', x, router_w) + router_b
            top_vals, top_idx = jax.lax.top_k(logits, top_k)
            keep = jax.nn.one_hot(top_idx, E, dtype=logits.dtype).sum(-2) > 0
            sparse_logits = jnp.where(keep, logits, NEG_INF)
            gating = jax.nn.softmax(sparse_logits, axis=-1)
            xf = x.reshape(-1, D)
            gf = gating.reshape(-1, E)
            h = jax.nn.relu(jnp.einsum('td,edh->eth', xf, w1) + b1[:, None, :])
            y = jnp.einsum('eth,ehd->etd', h, w2) + b2[:, None, :]
            out = jnp.einsum('etd,te->td', y, gf)
            return out.reshape(B, S, D)
        return _moe_forward(x, router_w, router_b, w1, b1, w2, b2, top_k=2)
    x = _layernorm(x + _L0_attn_ref(x, L0_attn_Wq, L0_attn_bq, L0_attn_Wk, L0_attn_bk, L0_attn_Wv, L0_attn_bv, L0_attn_Wo, L0_attn_bo), axis=-1)
    x = _layernorm(x + _L0_xattn_ref(x, ctx_1024, ctx_1024, L0_xattn_Wq, L0_xattn_Wk, L0_xattn_Wv, L0_xattn_Wo), axis=-1)
    x = _layernorm(x + _L0_ffn_ref(x, L0_ffn_switch_w, L0_ffn_switch_b, L0_ffn_w1, L0_ffn_b1, L0_ffn_w2, L0_ffn_b2), axis=-1)
    x = _layernorm(x + _L1_attn_ref(x, L1_attn_w_qkv, L1_attn_w_out, L1_attn_b_out), axis=-1)
    x = _layernorm(x + _L1_xattn_ref(x, ctx_1024, ctx_1024, fside_BxSx4_0, L1_xattn_Wq, L1_xattn_bq, L1_xattn_Wk, L1_xattn_bk, L1_xattn_Wv, L1_xattn_bv, L1_xattn_Wo, L1_xattn_bo, L1_xattn_Wg, L1_xattn_bg), axis=-1)
    x = _layernorm(x + _L1_ffn_ref(x, L1_ffn_router_w, L1_ffn_router_b, L1_ffn_w1, L1_ffn_b1, L1_ffn_w2, L1_ffn_b2), axis=-1)
    return x

_drawn_inputs = setup_inputs


def setup_inputs(seed=0):
    import zlib

    import numpy as np

    out = dict(_drawn_inputs(seed))
    spreads = {'L0_attn_bq': (0.0, 0.8),
     'L0_attn_bk': (0.0, 0.8),
     'L0_attn_bv': (0.0, 0.1),
     'L0_attn_bo': (0.0, 0.1),
     'L0_ffn_switch_b': (0.0, 0.1),
     'L0_ffn_b1': (0.0, 0.291),
     'L0_ffn_b2': (0.0, 0.1),
     'L1_xattn_bq': (0.0, 0.8),
     'L1_xattn_bk': (0.0, 0.8),
     'L1_xattn_bv': (0.0, 0.1),
     'L1_xattn_bo': (0.0, 0.1),
     'L1_xattn_bg': (0.0, 0.1),
     'L1_ffn_router_b': (0.0, 0.1),
     'L1_ffn_b1': (0.0, 0.357),
     'L1_ffn_b2': (0.0, 0.1)}
    factors = {'L0_attn_Wq': 8.0,
     'L0_attn_Wk': 8.0,
     'L0_attn_Wv': 4.306,
     'L1_xattn_Wq': 8.0,
     'L1_xattn_Wk': 8.0}
    for name, (base, spread) in spreads.items():
        noise = np.random.default_rng([zlib.crc32(name.encode()), seed]).standard_normal(out[name].shape)
        drawn = base * np.exp(spread * noise) if base else spread * noise
        out[name] = jnp.asarray(drawn.astype(out[name].dtype))
    for name, factor in factors.items():
        out[name] = (out[name] * factor).astype(out[name].dtype)
    return out
```

```python
from contextlib import ExitStack

import numpy as np

import concourse.bass as bass
from concourse import mybir

F32 = mybir.dt.float32
BF16 = mybir.dt.bfloat16
ALU = mybir.AluOpType
ACT = mybir.ActivationFunctionType
AX = mybir.AxisListType

NB = 32
S = 128
D = 128
H = 16
G = 4
HG = H // G
E = 8
F = 512
FC = F // 128
TB = 512
NT = NB * S // TB
TT = TB // S
EPS = 1e-5
CLIP = 1e-6
NEG = -1e30
TWO_PI_HI = 6.28125
TWO_PI_LO = 2 * np.pi - 6.28125
MAGIC = 1.5 * 2.0 ** 23
ANGLE_MAX = 3.1415925


class Core:

    def __init__(self, nc, stack, dram):
        self.nc = nc
        self.stack = stack
        self.dram = dram
        self.sems = []
        self.started = nc.alloc_semaphore("started")
        self.x_all = self.sb("x_all", [128, NB * D])
        self.xT_all = self.sb("xT_all", [128, NB * S])
        self.logits_all = self.sb("logits_all", [128, NB * E])
        self.ident = self.sb("ident", [128, 128])
        self.half_power = self.sb("half_power", [128, 4])
        self.eps_tile = self.sb("eps_tile", [128, 4])
        self.zeros = self.sb("zeros", [128, 1])
        self.half = self.sb("half", [128, 1])
        self.dve_mark = self.sb("dve_mark", [128, 1])

    def sb(self, name, shape, dt=F32, stack=None):
        return (stack or self.stack).enter_context(self.nc.sbuf_tensor(name, shape, dt))

    def ps(self, name, stack, shape=(128, 512), dt=F32):
        return stack.enter_context(self.nc.psum_tensor(name, list(shape), dt))

    def sem(self, name):
        handle = self.nc.alloc_semaphore(name)
        self.sems.append(handle)
        return handle

    def wait_apart(self, v, sem, value):
        v.wait_ge(sem, value)
        v.tensor_copy(self.dve_mark[:, :], self.eps_tile[:, 0:1])

    def end_phase(self):
        self.nc.clear_and_free_semaphores(self.sems)
        self.nc.all_engine_barrier()
        self.sems = []


def loads(n, b, par):
    return 8 * n * (b - par + 2)


def in_pairs(eng, batch, drain):
    batch(0, 0, 0, True)
    batch(1, 1, 1, True)
    with eng.Fori(0, NB // 2 - 2) as i:
        first = 2 * i + 2
        batch(first, 0, 2, True)
        batch(first + 1, 1, 2, True)
    batch(NB - 2, 0, 2, True)
    batch(NB - 1, 1, 2, False)
    drain()


def first_apart(eng, n, step):
    step(0)
    with eng.Fori(1, n) as i:
        step(i)


def broadcast_rows(ap, n):
    return bass.AP(tensor=ap.tensor, offset=ap.offset, ap=[[0, n]] + [list(p) for p in ap.ap])


def setup_phase(core):
    nc = core.nc
    s_consts = core.sem("consts_loaded")
    with nc.Block() as block:
        @block.sync
        def _(sp):
            sp.dma_start(core.ident[:, :], core.dram["identity"]).then_inc(s_consts, 16)
            sp.wait_ge(s_consts, 16)

        @block.gpsimd
        def _(pool):
            pool.memset(core.half_power[:, :], -0.5)
            pool.memset(core.zeros[:, :], 0.0)
            pool.memset(core.half[:, :], 0.5)
            pool.memset(core.eps_tile[:, :], EPS).then_inc(core.started, 1)
            pool.wait_ge(core.started, 1)


def geometry_phase(core, emb):
    nc, dram = core.nc, core.dram
    NJ = 8
    PB = NB // 2
    NQ = PB // 2
    W = 2 * NJ * S
    K = 64
    st = ExitStack()
    with st:
        sb = lambda n, shape: core.sb("geo_" + n, shape, stack=st)
        lo = sb("lo", [128, PB * S])
        hi = sb("hi", [128, PB * S])
        size = sb("size", [128, PB * S])
        lo_j = sb("lo_j", [128, PB * NJ])
        hi_j = sb("hi_j", [128, PB * NJ])
        size_j = sb("size_j", [128, PB * NJ])
        magic = sb("magic", [128, 2])
        quarter = sb("quarter", [128, 1])
        pos = sb("pos", [128, 2, W])
        turns = sb("turns", [128, 2, W])
        angle = sb("angle", [128, W])
        feat = sb("feat", [128, 2, 2, W])
        s_in = core.sem("geo_boxes_loaded")
        s_pre = core.sem("geo_prepared")
        s_prelog = core.sem("geo_log_sizes")
        s_d = core.sem("geo_distance_step")
        s_dist = core.sem("geo_distance_ready")
        s_a = core.sem("geo_log_step")
        s_turns = core.sem("geo_turns_ready")
        s_r = core.sem("geo_reduce_step")
        s_angle = core.sem("geo_angle_ready")
        s_abs = core.sem("geo_abs_ready")
        s_feat = core.sem("geo_features_ready")
        s_out = [core.sem(f"geo_stored{k}") for k in range(2)]

        def grid(t, q, rows):
            return t[0:rows, bass.ts(q, 2 * S)].rearrange("p (c a n) -> p c a n", c=2, a=1)\
                .broadcast_to([rows, 2, NJ, S])

        def cols(t, q, rows):
            return t[0:rows, bass.ts(q, 2 * NJ)].rearrange("p (c n a) -> p c n a", c=2, a=1)\
                .broadcast_to([rows, 2, NJ, S])

        def four(t, par, rows):
            return t[0:rows, par, :].rearrange("p (c n m) -> p c n m", c=2, n=NJ)

        def steps(eng, front, back):
            front(0, 0)
            front(1, 1)
            back(0, 0)
            with eng.Fori(1, NQ // 2) as i:
                front(2 * i, 0)
                back(2 * i - 1, 1)
                front(2 * i + 1, 1)
                back(2 * i, 0)
            back(NQ - 1, 1)

        with nc.Block() as block:
            @block.sync
            def _(sp):
                for kind in range(2):
                    for a in range(2):
                        for co in range(2):
                            p = 64 * kind + 32 * a + 16 * co
                            for t, side in ((lo, 0), (hi, 1)):
                                src = dram["boxesT"].rearrange("(i a) c n -> a c i n", a=2)[a, 2 * side + co]
                                sp.dma_start(t[p:p + 16, :].rearrange("p (b n) -> p b n", b=PB),
                                             broadcast_rows(src, 16)).then_inc(s_in, 16)
                sp.dma_start(lo_j[:, :], dram["boxes_lo_j"]).then_inc(s_in, 16)
                sp.dma_start(hi_j[:, :], dram["boxes_hi_j"]).then_inc(s_in, 16)

                def store(q, par):
                    sp.wait_ge(s_feat, q + 1)
                    for c in range(2):
                        for trig in range(2):
                            sp.dma_start(emb[bass.ds(2 * q + c, 1), trig, :, :].rearrange("a p n -> p (a n)"),
                                         feat[:, par, trig, c * NJ * S:(c + 1) * NJ * S])\
                                .then_inc(s_out[par], 16)
                with sp.Fori(0, NQ // 2) as i:
                    store(2 * i, 0)
                    store(2 * i + 1, 1)
                for par in range(2):
                    sp.wait_ge(s_out[par], 32 * NQ)

            @block.vector
            def _(v):
                v.wait_ge(s_in, 16 * 18)
                v.memset(magic[:, 0:1], MAGIC)
                v.memset(magic[:, 1:2], -MAGIC)
                v.memset(quarter[:, :], float(np.pi / 2))
                n = 0

                def did(ins):
                    nonlocal n
                    n += 1
                    ins.then_inc(s_pre, 1)
                    v.wait_ge(s_pre, n)

                did(v.tensor_tensor(size[:, :], hi[:, :], lo[:, :], ALU.subtract))
                did(v.tensor_tensor(size_j[:, :], hi_j[:, :], lo_j[:, :], ALU.subtract))
                did(v.tensor_scalar(size[:, :], size[:, :], 1.0, None, ALU.add))
                did(v.tensor_scalar(size_j[:, :], size_j[:, :], 1.0, None, ALU.add))
                did(v.tensor_tensor(lo[0:K, :], lo[0:K, :], hi[0:K, :], ALU.add))
                did(v.tensor_tensor(lo_j[0:K, :], lo_j[0:K, :], hi_j[0:K, :], ALU.add))
                did(v.tensor_scalar(lo[0:K, :], lo[0:K, :], 0.5, None, ALU.mult))
                did(v.tensor_scalar(lo_j[0:K, :], lo_j[0:K, :], 0.5, None, ALU.mult))
                did(v.reciprocal(size[0:K, :], size[0:K, :]))
                v.wait_ge(s_prelog, 2)

                def distance(q, par):
                    if not (isinstance(q, int) and q < 2):
                        v.wait_ge(s_angle, q - 1)
                    v.tensor_tensor(four(pos, par, 128), grid(lo, q, 128), cols(lo_j, q, 128), ALU.subtract)\
                        .then_inc(s_d, 1)
                    v.wait_ge(s_d, 3 * q + 1)
                    t = four(pos, par, K)
                    v.tensor_tensor(t, t, grid(size, q, K), ALU.mult).then_inc(s_d, 1)
                    v.wait_ge(s_d, 3 * q + 2)
                    t = pos[0:K, par, :]
                    v.scalar_tensor_tensor(out=t, in0=t, scalar=-1.0, in1=t, op0=ALU.mult, op1=ALU.max)\
                        .then_inc(s_d, 1)
                    v.wait_ge(s_d, 3 * q + 3)
                    v.tensor_scalar(t, t, 0.001, None, ALU.max).then_inc(s_dist, 1)

                def reduce(q, par):
                    v.wait_ge(s_turns, q + 1)
                    t, m = pos[:, par, :], turns[:, par, :]
                    v.scalar_tensor_tensor(out=t, in0=m, scalar=-TWO_PI_HI, in1=t, op0=ALU.mult, op1=ALU.add)\
                        .then_inc(s_r, 1)
                    v.wait_ge(s_r, 2 * q + 1)
                    v.scalar_tensor_tensor(out=t, in0=m, scalar=-TWO_PI_LO, in1=t, op0=ALU.mult, op1=ALU.add)\
                        .then_inc(s_r, 1)
                    v.wait_ge(s_r, 2 * q + 2)
                    if not (isinstance(q, int) and q == 0):
                        v.wait_ge(s_feat, q)
                    v.tensor_scalar(angle[:, :], t, ANGLE_MAX, -ANGLE_MAX, ALU.min, ALU.max)\
                        .then_inc(s_angle, 1)
                steps(v, distance, reduce)

            @block.scalar
            def _(act):
                act.wait_ge(s_pre, 4)
                act.activation(lo[K:128, :], size[K:128, :], ACT.Ln).then_inc(s_prelog, 1)
                act.activation(lo_j[K:128, :], size_j[K:128, :], ACT.Ln).then_inc(s_prelog, 1)

                def logs(q, par):
                    act.wait_ge(s_dist, q + 1)
                    act.activation(pos[0:K, par, :], pos[0:K, par, :], ACT.Ln).then_inc(s_a, 1)
                    act.wait_ge(s_a, 3 * q + 1)
                    act.activation(pos[:, par, :], pos[:, par, :], ACT.Copy, scale=100.0).then_inc(s_a, 1)
                    act.wait_ge(s_a, 3 * q + 2)
                    act.activation(turns[:, par, :], pos[:, par, :], ACT.Identity, bias=magic[:, 0:1],
                                   scale=float(1 / (2 * np.pi))).then_inc(s_a, 1)
                    act.wait_ge(s_a, 3 * q + 3)
                    act.activation(turns[:, par, :], turns[:, par, :], ACT.Identity, bias=magic[:, 1:2])\
                        .then_inc(s_turns, 1)

                def waves(q, par):
                    act.wait_ge(s_angle, q + 1)
                    if not (isinstance(q, int) and q < 2):
                        act.wait_ge(s_out[par], 32 * (q - par))
                    act.activation(feat[:, par, 0, :], angle[:, :], ACT.Sin)
                    act.activation(angle[:, :], angle[:, :], ACT.Abs).then_inc(s_abs, 1)
                    act.wait_ge(s_abs, q + 1)
                    act.activation(feat[:, par, 1, :], angle[:, :], ACT.Sin, bias=quarter[:, 0:1],
                                   scale=-1.0).then_inc(s_feat, 1)
                steps(act, logs, waves)


class Tail:

    def __init__(self, core, st, name, bias, router=None):
        self.core = core
        self.name = name
        self.bias = bias
        self.router = router
        self.res = core.sb(name + "_res", [128, D], stack=st)
        self.stats = core.sb(name + "_stats", [128, 6], stack=st)
        self.mv = core.sb(name + "_mv", [128, 2], stack=st)
        self.vpe = core.sb(name + "_vpe", [128, 1], stack=st)
        self.rstd = core.sb(name + "_rstd", [128, 1], stack=st)
        self.xn = core.sb(name + "_xn", [128, 2, D], stack=st)
        self.xs = core.sb(name + "_xTs", [128, S], stack=st)
        self.out_ready = core.sem(name + "_out_ready")
        self.res_step = core.sem(name + "_res_step")
        self.eps_added = core.sem(name + "_eps_added")
        self.rstd_ready = core.sem(name + "_rstd_ready")
        self.xn_ready = core.sem(name + "_xn_ready")
        self.xn_kept = core.sem(name + "_xn_kept")
        self.x_turned = core.sem(name + "_x_turned")
        self.x_moved = core.sem(name + "_x_moved")
        self.xT_kept = core.sem(name + "_xT_kept")
        self.logits_ready = core.sem(name + "_logits_ready")
        self.logits_moved = core.sem(name + "_logits_moved")

    def residual(self, v, b, y, x_in):
        k = 3 + (self.bias is not None)
        v.wait_ge(self.out_ready, b + 1)
        v.tensor_tensor(self.res[:, :], y, x_in, ALU.add).then_inc(self.res_step, 1)
        v.wait_ge(self.res_step, k * b + 1)
        if self.bias is not None:
            v.tensor_tensor(self.res[:, :], self.res[:, :], self.bias, ALU.add).then_inc(self.res_step, 1)
            v.wait_ge(self.res_step, k * b + 2)
        v.bn_stats(self.stats[:, :], self.res[:, :]).then_inc(self.res_step, 1)
        self.core.wait_apart(v, self.res_step, k * b + k - 1)
        v.bn_aggr(self.mv[:, :], self.stats[:, :]).then_inc(self.res_step, 1)

    def rsqrt(self, pool, b):
        k = 3 + (self.bias is not None)
        pool.wait_ge(self.res_step, k * b + k)
        pool.tensor_tensor(self.vpe[:, :], self.mv[:, 1:2], self.core.eps_tile[:, 0:1], ALU.add)\
            .then_inc(self.eps_added, 1)
        pool.wait_ge(self.eps_added, b + 1)
        pool.tensor_tensor(self.rstd[:, :], self.vpe[:, :], self.core.half_power[:, 0:1], ALU.pow)\
            .then_inc(self.rstd_ready, 1)

    def normalise(self, v, b, par):
        v.wait_ge(self.rstd_ready, b + 1)
        v.tensor_scalar(self.xn[:, par, :], self.res[:, :], self.mv[:, 0:1], self.rstd[:, 0:1],
                        ALU.subtract, ALU.mult).then_inc(self.xn_ready, 1)

    def keep(self, pool, b, par):
        pool.wait_ge(self.xn_ready, b + 1)
        pool.tensor_copy(self.core.x_all[:, bass.ts(b, D)], self.xn[:, par, :]).then_inc(self.xn_kept, 1)

    def turn_x(self, pe, b, par, bank):
        pe.wait_ge(self.xn_ready, b + 1)
        pe.transpose(bank[:, 0:S], self.xn[:, par, :], self.core.ident[:, :]).then_inc(self.x_turned, 1)

    def open_xT(self, pool):
        pool.memset(self.xs[:, :], 0.0).then_inc(self.xT_kept, 1)

    def move_xT(self, act, b, bank):
        act.wait_ge(self.x_turned, b + 1)
        act.wait_ge(self.xT_kept, b + 1)
        act.activation(self.xs[:, :], bank[:, 0:S], ACT.Copy).then_inc(self.x_moved, 1)

    def keep_T(self, pool, b):
        pool.wait_ge(self.x_moved, b + 1)
        pool.tensor_copy(self.core.xT_all[:, bass.ts(b, S)], self.xs[:, :]).then_inc(self.xT_kept, 1)

    def route(self, pe, b, bank):
        if self.router is None:
            return
        pe.wait_ge(self.x_moved, b + 1)
        pe.matmul(bank[:, S:S + E], self.xs[:, :], self.router[0], start=True, stop=True)\
            .then_inc(self.logits_ready, 1)

    def move_logits(self, v, b):
        if self.router is None:
            return
        v.wait_ge(self.logits_ready, b + 1)
        v.tensor_tensor(self.core.logits_all[:, bass.ts(b, E)], self.bank[:, S:S + E], self.router[1],
                        ALU.add).then_inc(self.logits_moved, 1)

    def bank_free(self, pe, b):
        pe.wait_ge(self.x_moved, b + 1)
        if self.router is not None:
            pe.wait_ge(self.logits_moved, b + 1)


def attention_phase(core, name, kind, hd, scale, out_bias, router, weights, emb=None):
    nc, dram = core.nc, core.dram
    rope, boxes = kind == "rope", kind == "boxes"
    HC = 128 // hd if not rope else 4
    NCH = H // HC
    CH = H * hd // 128
    VW = hd + 1
    NV = 4 if rope else H
    st = ExitStack()

    def head(g, i):
        return (HC * i + g) if rope else (8 * (g // 2) + 2 * i + g % 2)

    with st:
        sb = lambda n, shape, dt=F32: core.sb(f"{name}_{n}", shape, dt, stack=st)
        sem = lambda n: core.sem(f"{name}_{n}")
        bank_s = [core.ps(f"{name}_ps_scores{k}", st) for k in range(2)]
        bank_p = core.ps(f"{name}_ps_turned", st)
        bank_o = core.ps(f"{name}_ps_context", st)
        bank_j = [core.ps(f"{name}_ps_project{k}", st) for k in range(2)]
        bank_t = core.ps(f"{name}_ps_tail", st)
        bank_g = core.ps(f"{name}_ps_boxes", st)
        qT = sb("qT", [128, 2, NCH, S])
        kT = sb("kT", [128, 2, NCH, S])
        val = sb("val", [128, 2, NV, VW])
        shifted = sb("shifted", [128, 2, HG, S])
        probs = sb("probs", [128, G, HG, S])
        probsT = sb("probsT", [128, HG, S])
        top = sb("top", [128, 2, HG])
        inv = sb("inv", [128, HG])
        ctx = sb("ctx", [128, 2, H, hd])
        ctxT = sb("ctxT", [128, CH, S])
        wo = sb("wo", [128, CH, D])
        bias = sb("out_bias", [128, D]) if out_bias else None
        rw = sb("router_w", [128, E]) if router else None
        rb = sb("router_b", [128, E]) if router else None
        if rope:
            wqkv = sb("wqkv", [128, 192])
            bqkv = sb("bqkv", [128, 192])
            cos = sb("cos", [128, 8])
            sin = sb("sin", [128, 8])
            z = sb("z", [128, 192])
            zc = sb("zc", [128, 160])
            zs = sb("zs", [128, 160])
            qpad = sb("qpad", [128, H, 32])
            kpad = sb("kpad", [128, 4, 4, 32])
            src = sb("xT_in", [128, 2, S])
        else:
            wq = sb("wq", [128, H * hd])
            wk = sb("wk", [128, H * hd])
            wv = sb("wv", [128, H * hd])
            src = sb("cT_in", [128, 2, S])
        if boxes:
            bq = sb("bq", [128, NCH])
            bk = sb("bk", [128, NCH])
            bv = sb("bv", [128, CH])
            bv_wide = sb("bv_wide", [128, CH, 128])
            wbox = sb("wbox", [128, H, 16])
            KB = 96
            bg_rest = sb("bg_rest", [KB, H])
            bg_part = sb("bg_part", [KB, 3, H], BF16)
            bg_wide = sb("bg_wide", [KB, H, S], BF16)
            ones = sb("ones", [KB, 128], BF16)
            feats = sb("feats", [128, 2, 8, S])
            s_bg = sem("box_bias_step")
            s_feats = [sem(f"feats_loaded{k}") for k in range(2)]
            s_box = sem("box_weights_ready")
            s_gated = sem("gated")
            s_bias = sem("bias_step")
        tail = Tail(core, st, name, bias[:, :] if out_bias else None,
                    (rw[:, :], rb[:, :]) if router else None)
        tail.bank = bank_t
        s_w = sem("weights_loaded")
        s_x = sem("x_loaded")
        s_ones = sem("ones_ready")
        s_src = [sem(f"src_loaded{k}") for k in range(2)]
        s_prj = [sem("projected0"), sem("projected1")]
        s_mov = [sem("moved0"), sem("moved1")]
        s_rope = sem("rope_step")
        s_pad = sem("padded")
        s_scores = sem("scores_ready")
        s_top = sem("top_ready")
        s_shift = sem("shifted")
        s_exp = sem("exp_ready")
        s_turn = sem("probs_turned")
        s_pT = sem("probsT_ready")
        s_ctx = sem("context_ready")
        s_inv = sem("sums_inverted")
        s_norm = sem("context_scaled")
        s_cT = sem("context_turned")
        s_cTm = sem("contextT_ready")

        wl = []
        if rope:
            wl += [(wqkv[:, :], dram["a0_wqkv"]), (bqkv[:, :], broadcast_rows(dram["a0_bqkv"], 128)),
                   (cos[:, :], dram["rope_cos"]), (sin[:, :], dram["rope_sin"]),
                   (wo[:, 0, :], dram["a0_wo"]),
                   (bias[:, :], broadcast_rows(dram["a0_bo"], 128))]
        else:
            wl += [(wq[:, :], dram[weights + "_wq"]), (wk[:, :], dram[weights + "_wk"]),
                   (wv[:, :], dram[weights + "_wv"]),
                   (wo[:, :, :], dram[weights + "_wo"].rearrange("(c p) n -> p c n", p=128))]
        if boxes:
            wl += [(bq[:, :], dram["x1_bq"]), (bk[:, :], dram["x1_bk"]), (bv[:, :], dram["x1_bv"]),
                   (bias[:, :], broadcast_rows(dram["x1_bo"], 128)),
                   (wbox[:, :, :].rearrange("p h j -> p (h j)"), dram["x1_wbox_sel"]),
                   (bg_rest[:, :], broadcast_rows(dram["x1_bg"], KB))]
        if router:
            wl += [(rw[:, :], dram[router + "_w"]), (rb[:, :], broadcast_rows(dram[router + "_b"], 128))]
        n_w = len(wl)
        HALVES = 1 if rope else 2
        FILLS = [2, 1] if rope else [3, 3]

        with nc.Block() as block:
            @block.sync
            def _(sp):
                for t, source in wl:
                    sp.dma_start(t, source).then_inc(s_w, 16)

                def load(half, par, wait):
                    b = 2 * half + par
                    if wait:
                        sp.wait_ge(s_box if boxes else s_prj[1], (G if boxes else FILLS[1]) * (b - 1))
                    if rope:
                        sp.dma_start(src[:, par, :], dram["xT"][bass.ds(b, 1), :, :]
                                     .rearrange("a p n -> p (a n)")).then_inc(s_src[par], 16)
                    else:
                        sp.dma_start(src[:, par, :], dram["ctxT"][bass.ds(b, 1), :, :]
                                     .rearrange("a p n -> p (a n)")).then_inc(s_src[par], 16)
                    if boxes:
                        for trig in range(2):
                            for kind in range(2):
                                p, r = 64 * trig + 32 * kind, 64 * kind + 32 * par
                                sp.dma_start(feats[p:p + 32, par, :, :].rearrange("p a n -> p (a n)"),
                                             emb[bass.ds(half, 1), trig, r:r + 32, :]
                                             .rearrange("a p n -> p (a n)")).then_inc(s_feats[par], 16)

                load(0, 0, False)
                load(0, 1, False)
                if rope:
                    sp.dma_start(core.x_all[:, :].rearrange("p (b n) -> p b n", b=NB),
                                 dram["x"].rearrange("b p n -> p b n")).then_inc(s_x, 16)
                with sp.Fori(1, NB // 2) as i:
                    load(i, 0, True)
                    load(i, 1, True)

            @block.tensor
            def _(pe):
                def fill(k, b, n):
                    if isinstance(b, int) and FILLS[k] * b + n == 0:
                        return
                    pe.wait_ge(s_mov[k], FILLS[k] * b + n)

                def project(b, par, part):
                    if rope:
                        if part == 0:
                            pe.wait_ge(s_src[par], loads(1, b, par))
                            fill(0, b, 0)
                            pe.matmul(bank_j[0][:, 0:192], src[:, par, :], wqkv[:, :], start=True, stop=True)\
                                .then_inc(s_prj[0], 1)
                        if part == 2:
                            pe.wait_ge(s_pad, b + 1)
                            fill(1, b, 0)
                            for r in range(4):
                                mm = pe.transpose(bank_j[1][:, r * S:(r + 1) * S],
                                                  qpad[:, 4 * r:4 * r + 4, :].rearrange("p h d -> p (h d)"),
                                                  core.ident[:, :])
                            mm.then_inc(s_prj[1], 1)
                            fill(0, b, 1)
                            for r in range(4):
                                mm = pe.transpose(bank_j[0][:, r * S:(r + 1) * S],
                                                  kpad[:, r, :, :].rearrange("p h d -> p (h d)"),
                                                  core.ident[:, :])
                            mm.then_inc(s_prj[0], 1)
                        return
                    if part == 0:
                        pe.wait_ge(s_src[par], loads(1, b, par))
                    if part == 3:
                        return
                    for k in range(2):
                        fill(k, b, part)
                        if part < 2:
                            w = wq if part == 0 else wk
                            xr = core.xT_all[:, bass.ts(b, S)] if part == 0 else src[:, par, :]
                            for cc in range(4):
                                c = 4 * k + cc
                                mm = pe.matmul(bank_j[k][:, cc * S:(cc + 1) * S], w[:, c * 128:(c + 1) * 128],
                                               xr, start=True, stop=True)
                        else:
                            mm = pe.matmul(bank_j[k][:, :], src[:, par, :], wv[:, k * 512:(k + 1) * 512],
                                           start=True, stop=True)
                        mm.then_inc(s_prj[k], 1)

                def scores(b, par, g, first):
                    t = G * b + g
                    pe.wait_ge(s_mov[0], FILLS[0] * (b + 1) - (0 if rope else 1))
                    pe.wait_ge(s_mov[1], FILLS[1] * (b + 1) - (0 if rope else 1))
                    if not (first and g < 2):
                        pe.wait_ge(s_shift, t - 1)
                    for i in range(HG):
                        h = head(g, i)
                        c, r = h // HC, 128 // HC * (h % HC)
                        mm = pe.matmul(bank_s[g % 2][:, i * S:(i + 1) * S], qT[r:r + hd, par, c, :],
                                       kT[r:r + hd, par, c, :], start=True, stop=True)
                    mm.then_inc(s_scores, 1)
                    if boxes:
                        if g == 0:
                            pe.wait_ge(s_feats[par], loads(4, b, par))
                        if not (first and g == 0):
                            pe.wait_ge(s_gated, t)
                        h0 = head(g, 0)
                        pe.matmul(bank_g[:, :].rearrange("p (h n) -> p h n", h=HG), ones[:, :],
                                  bg_wide[:, h0:h0 + 7:2, :], start=True, stop=False,
                                  skip_group_check=True)
                        for J in range(8):
                            out = bank_g[:, :].rearrange("p (h j) -> p h j", h=HG)[:, :, 16 * J:16 * J + 16]
                            mm = pe.matmul(out, feats[:, par, J, :], wbox[:, h0:h0 + 7:2, :],
                                           start=False, stop=(J == 7), skip_group_check=True)
                        mm.then_inc(s_box, 1)

                def turn_probs(b, g):
                    t = G * b + g
                    pe.wait_ge(s_gated if boxes else s_exp, t + 1)
                    if not (isinstance(t, int) and t == 0):
                        pe.wait_ge(s_pT, t)
                    for i in range(HG):
                        mm = pe.transpose(bank_p[:, i * S:(i + 1) * S], probs[:, g, i, :],
                                          core.ident[:, :])
                    mm.then_inc(s_turn, 1)

                def weigh_values(b, par, g):
                    t = G * b + g
                    pe.wait_ge(s_pT, t + 1)
                    if not (isinstance(t, int) and t == 0):
                        pe.wait_ge(s_norm, t)
                    if g == 0 and not rope:
                        pe.wait_ge(s_mov[0], FILLS[0] * (b + 1))
                        pe.wait_ge(s_mov[1], FILLS[1] * (b + 1))
                    for i in range(HG):
                        hv = i if rope else head(g, i)
                        mm = pe.matmul(bank_o[:, i * VW:(i + 1) * VW], probsT[:, i, :], val[:, par, hv, :],
                                       start=True, stop=True)
                    mm.then_inc(s_ctx, 1)

                def turn_context(b, par, half, back):
                    if rope:
                        pe.wait_ge(s_norm, G * b + 4)
                        cs = range(1)
                    else:
                        pe.wait_ge(s_norm, G * b + 2 * half + 2)
                        cs = range(4 * half, 4 * half + 4)
                    if half == 0 and back >= 1:
                        pe.wait_ge(tail.res_step, tail_k * b - tail_k + 1)
                    if half == 1 and back >= 1:
                        tail.bank_free(pe, b - 1)
                    for c in cs:
                        mm = pe.transpose(bank_t[:, (c % 4) * S:(c % 4 + 1) * S],
                                          ctx[:, par, :, :].rearrange("p h d -> p (h d)")
                                          [:, c * 128:(c + 1) * 128], core.ident[:, :])
                    mm.then_inc(s_cT, 1)

                tail_k = 3 + (bias is not None)

                def project_out(b):
                    pe.wait_ge(s_cTm, HALVES * (b + 1))
                    for c in range(CH):
                        mm = pe.matmul(bank_t[:, 0:D], ctxT[:, c, :], wo[:, c, :], start=(c == 0),
                                       stop=(c == CH - 1))
                    mm.then_inc(tail.out_ready, 1)

                def turn_x(b, par, half0_next):
                    if half0_next:
                        pe.wait_ge(s_cTm, HALVES * (b + 1) + 1)
                    else:
                        pe.wait_ge(tail.res_step, tail_k * b + 1)
                    tail.turn_x(pe, b, par, bank_t)

                def batch(b, par, back, more, here=True):
                    for g in range(G):
                        if here:
                            scores(b, par, g, back == 0)
                        if g == 0 and back == 2:
                            project_out(b - 2)
                        if g == 3 and here:
                            weigh_values(b, par, 0)
                        elif g < 3 and back:
                            weigh_values(b - 1, 1 - par, g + 1)
                        if g == 3 and back == 2:
                            tail.route(pe, b - 2, bank_t)
                        if g >= 2 and here:
                            turn_probs(b, g - 2)
                        elif g < 2 and back:
                            turn_probs(b - 1, g + 2)
                        if more:
                            project(b + 1, 1 - par, g)
                        if g == 1 and back and not rope:
                            turn_context(b - 1, 1 - par, 0, back - 1)
                        if g == 2 and back == 2:
                            turn_x(b - 2, par, not rope)
                        if g == 3 and back:
                            turn_context(b - 1, 1 - par, 1, back - 1)

                def drain():
                    batch(NB, 0, 2, False, False)
                    b, par = NB - 1, 1
                    project_out(b)
                    turn_x(b, par, False)
                    tail.route(pe, b, bank_t)

                pe.wait_ge(s_w, 16 * n_w)
                if boxes:
                    pe.wait_ge(s_bias, 1)
                    for c in range(CH):
                        mm = pe.matmul(bank_t[:, 0:D], bv_wide[:, c, :], wo[:, c, :], start=(c == 0),
                                       stop=(c == CH - 1))
                    mm.then_inc(s_bias, 1)
                    pe.wait_ge(s_bias, 3)
                    pe.wait_ge(s_bg, 10)
                for part in range(4):
                    project(0, 0, part)
                in_pairs(pe, batch, drain)

            @block.vector
            def _(v):
                v.wait_ge(s_w, 16 * n_w)
                v.memset(val[:, :, :, hd:VW], 1.0).then_inc(s_ones, 1)
                if rope:
                    v.memset(qpad[:, :, :], 0.0).then_inc(s_ones, 1)
                    v.memset(kpad[:, :, :, :], 0.0).then_inc(s_ones, 1)
                    v.wait_ge(s_ones, 3)
                if boxes:
                    v.tensor_copy(bv_wide[:, :, :], bv[:, :].rearrange("p (c a) -> p c a", a=1)
                                  .broadcast_to([128, CH, 128])).then_inc(s_bias, 1)
                    v.wait_ge(s_bias, 2)
                    v.tensor_tensor(bias[:, :], bias[:, :], bank_t[:, 0:D], ALU.add).then_inc(s_bias, 1)
                    v.memset(ones[:, :], 1.0).then_inc(s_bg, 1)
                    v.memset(bg_wide[:, :, :], 0.0).then_inc(s_bg, 1)
                    n = 2
                    for part in range(3):
                        v.tensor_copy(bg_part[:, part, :], bg_rest[:, :]).then_inc(s_bg, 1)
                        n += 1
                        v.wait_ge(s_bg, n)
                        if part < 2:
                            v.tensor_tensor(bg_rest[:, :], bg_rest[:, :], bg_part[:, part, :], ALU.subtract)\
                                .then_inc(s_bg, 1)
                            n += 1
                            v.wait_ge(s_bg, n)
                    for part in range(3):
                        r = 32 * part
                        v.tensor_copy(bg_wide[r:r + 1, :, :],
                                      bg_part[r:r + 1, part, :].rearrange("p (h n) -> p h n", n=1)
                                      .broadcast_to([1, H, S])).then_inc(s_bg, 1)

                def rotate(b, par):
                    R = 6
                    v.wait_ge(s_prj[0], 2 * b + 1)
                    v.tensor_tensor(z[:, :], bank_j[0][:, 0:192], bqkv[:, :], ALU.add).then_inc(s_mov[0], 1)
                    v.wait_ge(s_mov[0], 2 * b + 1)
                    z3 = z[:, 0:160].rearrange("p (h d) -> p h d", d=8)
                    zc3 = zc[:, :].rearrange("p (h d) -> p h d", d=8)
                    zs3 = zs[:, :].rearrange("p (h d) -> p h d", d=8)

                    def wide(t, a, e):
                        return t[:, a:e].rearrange("p (a d) -> p a d", a=1).broadcast_to([128, 20, e - a])
                    v.tensor_tensor(zc3, z3, wide(cos, 0, 8), ALU.mult)
                    v.tensor_tensor(zs3[:, :, 0:4], z3[:, :, 1:8:2], wide(sin, 0, 4), ALU.mult)
                    v.tensor_tensor(zs3[:, :, 4:8], z3[:, :, 0:8:2], wide(sin, 4, 8), ALU.mult)\
                        .then_inc(s_rope, 1)
                    v.wait_ge(s_rope, b + 1)
                    v.tensor_tensor(qpad[:, :, 0:8], zc3[:, 0:16, :], zs3[:, 0:16, :], ALU.add)

                    def four(t3):
                        return t3[:, 16:20, :].rearrange("p (k a) d -> p k a d", a=1)\
                            .broadcast_to([128, 4, 4, 8])
                    v.tensor_tensor(kpad[:, :, :, 0:8], four(zc3), four(zs3), ALU.add).then_inc(s_pad, 1)

                def empty(b, par, part):
                    if rope:
                        if part == 0:
                            rotate(b, par)
                        if part == 2:
                            v.wait_ge(s_prj[1], b + 1)
                            v.tensor_copy(val[:, par, :, 0:hd], z[:, 160:192].rearrange("p (h d) -> p h d", d=8))
                            v.tensor_copy(qT[:, par, :, :].rearrange("p c n -> p (c n)"), bank_j[1][:, :])\
                                .then_inc(s_mov[1], 1)
                        return
                    if part == 3:
                        return
                    v.wait_ge(s_prj[1], 3 * b + part + 1)
                    dst = (qT, kT)[part][:, par, 4:8, :] if part < 2 else val[:, par, 8:16, 0:hd]
                    if boxes and part < 2:
                        bb = (bq, bk)[part][:, 4:8].rearrange("p (c a) -> p c a", a=1)\
                            .broadcast_to([128, 4, S])
                        v.tensor_tensor(dst, bank_j[1][:, :].rearrange("p (c n) -> p c n", c=4), bb, ALU.add)\
                            .then_inc(s_mov[1], 1)
                    elif part < 2:
                        v.tensor_copy(dst.rearrange("p c n -> p (c n)"), bank_j[1][:, :]).then_inc(s_mov[1], 1)
                    else:
                        v.tensor_copy(dst, bank_j[1][:, :].rearrange("p (h d) -> p h d", d=hd))\
                            .then_inc(s_mov[1], 1)

                def gate(b, g):
                    t = G * b + g
                    v.wait_ge(s_exp, t + 1)
                    v.wait_ge(s_box, t + 1)
                    p = probs[:, g, :, :].rearrange("p h n -> p (h n)")
                    v.scalar_tensor_tensor(out=p, in0=bank_g[:, :], scalar=CLIP, in1=p,
                                           op0=ALU.max, op1=ALU.mult).then_inc(s_gated, 1)

                def shift(b, g, first):
                    t = G * b + g
                    sc = bank_s[g % 2][:, :].rearrange("p (h n) -> p h n", h=HG)
                    v.wait_ge(s_scores, t + 1)
                    v.tensor_reduce(top[:, g % 2, :], sc, AX.X, ALU.max).then_inc(s_top, 1)
                    v.wait_ge(s_top, t + 1)
                    if not (first and g < 2):
                        v.wait_ge(s_exp, t - 1)
                    v.tensor_tensor(shifted[:, g % 2, :, :], sc,
                                    top[:, g % 2, :].rearrange("p (h a) -> p h a", a=1)
                                    .broadcast_to([128, HG, S]), ALU.subtract).then_inc(s_shift, 1)

                def scale_context(b, par, g):
                    t = G * b + g
                    o3 = bank_o[:, 0:HG * VW].rearrange("p (h d) -> p h d", d=VW)
                    v.wait_ge(s_ctx, t + 1)
                    v.reciprocal(inv[:, :].rearrange("p (h a) -> p h a", a=1), o3[:, :, hd:VW])\
                        .then_inc(s_inv, 1)
                    v.wait_ge(s_inv, t + 1)
                    h0, step = (g, 4) if rope else (head(g, 0), 2)
                    v.tensor_tensor(ctx[:, par, h0:h0 + step * (HG - 1) + 1:step, :], o3[:, :, 0:hd],
                                    inv[:, :].rearrange("p (h a) -> p h a", a=1)
                                    .broadcast_to([128, HG, hd]), ALU.mult).then_inc(s_norm, 1)

                def residual(b, par):
                    if rope and isinstance(b, int) and b == 0:
                        v.wait_ge(s_x, 16)
                    tail.residual(v, b, bank_t[:, 0:D], core.x_all[:, bass.ts(b, D)])

                def batch(b, par, back, more, here=True):
                    for g in range(G):
                        if g == 1 and back == 2:
                            residual(b - 2, par)
                        if here:
                            shift(b, g, back == 0)
                        if g == 2 and back == 2:
                            tail.normalise(v, b - 2, par)
                        if g == 3 and back == 2:
                            tail.move_logits(v, b - 2)
                        if g == 3 and here:
                            scale_context(b, par, 0)
                        elif g < 3 and back:
                            scale_context(b - 1, 1 - par, g + 1)
                        if boxes and here:
                            gate(b, g)
                        if more:
                            empty(b + 1, 1 - par, g)

                def drain():
                    batch(NB, 0, 2, False, False)
                    b, par = NB - 1, 1
                    residual(b, par)
                    tail.normalise(v, b, par)
                    tail.move_logits(v, b)

                for part in range(4):
                    empty(0, 0, part)
                in_pairs(v, batch, drain)

            @block.scalar
            def _(act):
                def empty(b, par, part):
                    if rope:
                        if part == 2:
                            act.wait_ge(s_prj[0], 2 * b + 2)
                            act.activation(kT[:, par, :, :].rearrange("p c n -> p (c n)"), bank_j[0][:, :],
                                           ACT.Copy).then_inc(s_mov[0], 1)
                        return
                    if part == 3:
                        return
                    act.wait_ge(s_prj[0], 3 * b + part + 1)
                    if part == 2:
                        act.activation(val[:, par, 0:8, 0:hd],
                                       bank_j[0][:, :].rearrange("p (h d) -> p h d", d=hd), ACT.Copy)\
                            .then_inc(s_mov[0], 1)
                        return
                    dst = (qT, kT)[part]
                    if not boxes:
                        act.activation(dst[:, par, 0:4, :].rearrange("p c n -> p (c n)"), bank_j[0][:, :],
                                       ACT.Copy).then_inc(s_mov[0], 1)
                        return
                    for c in range(4):
                        ins = act.activation(dst[:, par, c, :], bank_j[0][:, c * S:(c + 1) * S], ACT.Identity,
                                             bias=(bq, bk)[part][:, c:c + 1])
                    ins.then_inc(s_mov[0], 1)

                def move_probs(b, g):
                    act.wait_ge(s_turn, G * b + g + 1)
                    act.activation(probsT[:, :, :].rearrange("p h n -> p (h n)"), bank_p[:, :], ACT.Copy)\
                        .then_inc(s_pT, 1)

                def exponentials(b, g, first):
                    t = G * b + g
                    act.wait_ge(s_shift, t + 1)
                    if not first:
                        act.wait_ge(s_turn, t - 3)
                    act.activation(probs[:, g, :, :].rearrange("p h n -> p (h n)"),
                                   shifted[:, g % 2, :, :].rearrange("p h n -> p (h n)"), ACT.Exp,
                                   scale=scale).then_inc(s_exp, 1)

                def move_context(b, half):
                    act.wait_ge(s_cT, HALVES * b + half + 1)
                    n = CH // HALVES
                    act.activation(ctxT[:, n * half:n * half + n, :].rearrange("p c n -> p (c n)"),
                                   bank_t[:, 0:n * S], ACT.Copy).then_inc(s_cTm, 1)

                def batch(b, par, back, more, here=True):
                    for g in range(G):
                        if here:
                            exponentials(b, g, back == 0)
                        if g >= 2 and here:
                            move_probs(b, g - 2)
                        elif g < 2 and back:
                            move_probs(b - 1, g + 2)
                        if more:
                            empty(b + 1, 1 - par, g)
                        if g == 1 and back and not rope:
                            move_context(b - 1, 0)
                        if g == 2 and back == 2:
                            tail.move_xT(act, b - 2, bank_t)
                        if g == 3 and back:
                            move_context(b - 1, HALVES - 1)

                def drain():
                    batch(NB, 0, 2, False, False)
                    tail.move_xT(act, NB - 1, bank_t)

                for part in range(4):
                    empty(0, 0, part)
                in_pairs(act, batch, drain)

            @block.gpsimd
            def _(pool):
                pool_batches(pool, tail)


def pool_batches(pool, tail):
    tail.open_xT(pool)

    def batch(b, par):
        tail.rsqrt(pool, b)
        tail.keep(pool, b, par)
        tail.keep_T(pool, b)

    def pair(i):
        batch(2 * i, 0)
        batch(2 * i + 1, 1)
    first_apart(pool, NB // 2, pair)


def expert_phase(core, name, top2, out):
    nc, dram = core.nc, core.dram
    st = ExitStack()
    with st:
        sb = lambda n, shape, dt=F32: core.sb(f"{name}_{n}", shape, dt, stack=st)
        sem = lambda n: core.sem(f"{name}_{n}")
        w1 = sb("w1", [128, E, F])
        w2 = sb("w2", [128, E, FC, D])
        b1 = sb("b1", [128, E, FC])
        b2 = sb("b2", [E, D])
        order = sb("order", [128, E])
        hid = sb("hid", [128, 2, FC, TB])
        acc = sb("acc", [128, TT, D])
        gates = sb("gates", [128, NB, E])
        gcur = sb("gcur", [128, TT, E])
        gT = sb("gT", [E, TB])
        t_a = sb("t_a", [128, NB, E])
        t_b = sb("t_b", [128, NB, E])
        m_a = sb("m_a", [128, NB])
        m_b = sb("m_b", [128, NB])
        m_c = sb("m_c", [128, NB])
        t_c = sb("t_c", [128, NB, E])
        stats = sb("stats", [128, TT, 6])
        mv = sb("mv", [128, TT, 2])
        vpe = sb("vpe", [128, TT])
        rstd = sb("rstd", [128, TT])
        bank_h = [core.ps(f"{name}_ps_h{k}", st) for k in range(FC)]
        bank_y = [core.ps(f"{name}_ps_y{k}", st) for k in range(2)]
        bank_g = core.ps(f"{name}_ps_gT", st)
        bank_b = core.ps(f"{name}_ps_bias", st)
        s_w = sem("weights_loaded")
        s_gs = sem("gate_step")
        s_gexp = sem("gate_exp")
        s_gcur = sem("gates_copied")
        s_gt = sem("gates_turned")
        s_gT = sem("gatesT_ready")
        s_b2 = sem("bias_ready")
        s_h = sem("hidden_ready")
        s_a = sem("activated")
        s_y = sem("y_ready")
        s_acc = sem("accumulated")
        s_ln = sem("norm_step")
        s_eps = sem("eps_added")
        s_rs = sem("rstd_ready")
        s_xn = sem("xn_ready")
        s_out = sem("stored")
        func = ACT.Relu if top2 else ACT.Gelu_apprx_tanh
        wp = "f1" if top2 else "f0"

        with nc.Block() as block:
            @block.sync
            def _(sp):
                sp.dma_start(b1[:, :, :].rearrange("p e c -> p (e c)"), dram[wp + "_b1"]).then_inc(s_w, 16)
                sp.dma_start(b2[:, :], dram[wp + "_b2"]).then_inc(s_w, 16)
                sp.dma_start(order[:, :], broadcast_rows(dram["order"], 128)).then_inc(s_w, 16)
                for e in range(E):
                    sp.dma_start(w1[:, e, :], dram[wp + "_w1"][e]).then_inc(s_w, 16)
                    sp.dma_start(w2[:, e, :, :], dram[wp + "_w2"][e].rearrange("(c p) n -> p c n", p=128))\
                        .then_inc(s_w, 16)
                if out is not None:
                    with sp.Fori(0, NT) as i:
                        sp.wait_ge(s_xn, i + 1)
                        sp.dma_start(out[bass.ts(i, TT), :, :].rearrange("b p n -> p b n"),
                                     core.x_all[:, bass.ts(i, TB)].rearrange("p (b n) -> p b n", b=TT))\
                            .then_inc(s_out, 16)
                    sp.wait_ge(s_out, 16 * NT)

            @block.tensor
            def _(pe):
                def values(i, e):
                    pe.wait_ge(s_a, FC * E * i + FC * (e + 1))
                    if e >= 2 or not isinstance(i, int):
                        pe.wait_ge(s_acc, E * i + e - 1)
                    for t in range(TT):
                        for c in range(FC):
                            mm = pe.matmul(bank_y[e % 2][:, t * D:(t + 1) * D],
                                           hid[:, e % 2, c, t * S:(t + 1) * S], w2[:, e, c, :],
                                           start=(c == 0), stop=(c == FC - 1))
                    mm.then_inc(s_y, 1)

                pe.wait_ge(s_w, 16 * (3 + 2 * E))

                def tokens(i):
                    for e in range(E):
                        for c in range(FC):
                            if e > 0 or not isinstance(i, int):
                                pe.wait_ge(s_a, FC * E * i + FC * (e - 1) + c + 1)
                            pe.matmul(bank_h[c][:, :], w1[:, e, c * 128:(c + 1) * 128],
                                      core.xT_all[:, bass.ts(i, TB)], start=True, stop=True).then_inc(s_h, 1)
                        if e == 0:
                            pe.wait_ge(s_gcur, i + 1)
                            for t in range(TT):
                                mm = pe.transpose(bank_g[0:E, t * S:(t + 1) * S], gcur[:, t, :],
                                                  core.ident[:, :])
                            mm.then_inc(s_gt, 1)
                        else:
                            values(i, e - 1)
                        if e == 1:
                            pe.wait_ge(s_gT, i + 1)
                            for t in range(TT):
                                mm = pe.matmul(bank_b[:, t * D:(t + 1) * D], gT[:, t * S:(t + 1) * S],
                                               b2[:, :], start=True, stop=True)
                            mm.then_inc(s_b2, 1)
                    values(i, E - 1)
                first_apart(pe, NT, tokens)

            @block.scalar
            def _(act):
                if top2:
                    act.wait_ge(s_gs, 13)
                    act.activation(m_b[:, :], m_c[:, :], ACT.Exp).then_inc(s_gexp, 1)
                else:
                    act.wait_ge(s_gs, 6)
                    act.activation(t_b[:, :, :], t_a[:, :, :], ACT.Exp).then_inc(s_gexp, 1)
                act.wait_ge(s_w, 16 * (3 + 2 * E))
                with act.Fori(0, NT) as i:
                    for e in range(E):
                        for c in range(FC):
                            act.wait_ge(s_h, FC * (E * i + e) + c + 1)
                            act.activation(hid[:, e % 2, c, :], bank_h[c][:, :], func,
                                           bias=b1[:, e, c:c + 1]).then_inc(s_a, 1)

            @block.vector
            def _(v):
                n = 0

                def did(ins):
                    nonlocal n
                    n += 1
                    ins.then_inc(s_gs, 1)
                    v.wait_ge(s_gs, n)

                v.wait_ge(s_w, 16 * (3 + 2 * E))
                lg = core.logits_all[:, :].rearrange("p (b e) -> p b e", e=E)

                def wide(t):
                    return t[:, :].rearrange("p (b a) -> p b a", a=1).broadcast_to([128, NB, E])
                rank = order[:, :].rearrange("p (a e) -> p a e", a=1).broadcast_to([128, NB, E])

                def first_of_largest(src_, top, pick, tmp, mt):
                    did(v.tensor_reduce(top[:, :], src_, AX.X, ALU.max))
                    did(v.tensor_tensor(pick[:, :, :], src_, wide(top), ALU.is_equal))
                    did(v.tensor_tensor(tmp[:, :, :], pick[:, :, :], rank, ALU.mult))
                    did(v.tensor_reduce(mt[:, :], tmp[:, :, :], AX.X, ALU.max))
                    did(v.tensor_tensor(pick[:, :, :], tmp[:, :, :], wide(mt), ALU.is_equal))

                first_of_largest(lg, m_a, gates, t_a, m_b)
                if not top2:
                    did(v.tensor_tensor(t_a[:, :, :], lg, wide(m_a), ALU.subtract))
                    v.wait_ge(s_gexp, 1)
                    did(v.tensor_reduce(m_b[:, :], t_b[:, :, :], AX.X, ALU.add))
                    did(v.reciprocal(m_b[:, :], m_b[:, :]))
                    did(v.tensor_tensor(gates[:, :, :], gates[:, :, :], wide(m_b), ALU.mult))
                else:
                    did(v.tensor_scalar(t_a[:, :, :], gates[:, :, :], NEG, None, ALU.mult))
                    did(v.tensor_tensor(t_b[:, :, :], t_a[:, :, :], lg, ALU.add))
                    first_of_largest(t_b[:, :, :], m_c, t_c, t_a, m_b)
                    did(v.tensor_tensor(m_c[:, :], m_c[:, :], m_a[:, :], ALU.subtract))
                    v.wait_ge(s_gexp, 1)
                    did(v.tensor_scalar(m_a[:, :], m_b[:, :], 1.0, None, ALU.add))
                    did(v.reciprocal(m_a[:, :], m_a[:, :]))
                    did(v.tensor_tensor(m_b[:, :], m_b[:, :], m_a[:, :], ALU.mult))
                    did(v.tensor_tensor(gates[:, :, :], gates[:, :, :], wide(m_a), ALU.mult))
                    did(v.tensor_tensor(t_c[:, :, :], t_c[:, :, :], wide(m_b), ALU.mult))
                    did(v.tensor_tensor(gates[:, :, :], gates[:, :, :], t_c[:, :, :], ALU.add))

                def tokens(i):
                    if not isinstance(i, int):
                        v.wait_ge(s_gt, i)
                    v.tensor_copy(gcur[:, :, :].rearrange("p t e -> p (t e)"),
                                  gates[:, :, :].rearrange("p b e -> p (b e)")[:, bass.ts(i, TT * E)])\
                        .then_inc(s_gcur, 1)
                    v.wait_ge(s_gt, i + 1)
                    v.tensor_copy(gT[:, :], bank_g[0:E, :]).then_inc(s_gT, 1)
                    v.wait_ge(s_b2, i + 1)
                    v.tensor_tensor(acc[:, :, :].rearrange("p t d -> p (t d)"), bank_b[:, :],
                                    core.x_all[:, bass.ts(i, TB)], ALU.add).then_inc(s_ln, 1)
                    v.wait_ge(s_ln, 3 * i + 1)
                    for e in range(E):
                        v.wait_ge(s_y, E * i + e + 1)
                        if e > 0:
                            v.wait_ge(s_acc, E * i + e)
                        for t in range(TT):
                            ins = v.scalar_tensor_tensor(
                                out=acc[:, t, :], in0=bank_y[e % 2][:, t * D:(t + 1) * D],
                                scalar=gcur[:, t, e:e + 1], in1=acc[:, t, :], op0=ALU.mult, op1=ALU.add)
                        ins.then_inc(s_acc, 1)
                    v.wait_ge(s_acc, E * i + E)
                    for t in range(TT):
                        ins = v.bn_stats(stats[:, t, :], acc[:, t, :])
                    ins.then_inc(s_ln, 1)
                    core.wait_apart(v, s_ln, 3 * i + 2)
                    for t in range(TT):
                        ins = v.bn_aggr(mv[:, t, :], stats[:, t, :])
                    ins.then_inc(s_ln, 1)
                    v.wait_ge(s_rs, i + 1)
                    for t in range(TT):
                        ins = v.tensor_scalar(core.x_all[:, bass.ds(i * TB + t * D, D)], acc[:, t, :],
                                              mv[:, t, 0:1], rstd[:, t:t + 1], ALU.subtract, ALU.mult)
                    ins.then_inc(s_xn, 1)
                first_apart(v, NT, tokens)

            @block.gpsimd
            def _(pool):
                with pool.Fori(0, NT) as i:
                    pool.wait_ge(s_ln, 3 * i + 3)
                    pool.tensor_tensor(vpe[:, :], mv[:, :, 1], core.eps_tile[:, :], ALU.add).then_inc(s_eps, 1)
                    pool.wait_ge(s_eps, i + 1)
                    pool.tensor_tensor(rstd[:, :], vpe[:, :], core.half_power[:, :], ALU.pow).then_inc(s_rs, 1)


def block_attention_phase(core):
    nc, dram = core.nc, core.dram
    name, HD, CH = "l1a", 64, 8
    QX, KX = 64, 96
    QW, KW = QX + S, S + KX
    VW = HD + 4
    FILLS = 10
    TAIL_STEPS = 4
    st = ExitStack()
    with st:
        sb = lambda n, shape, dt=F32: core.sb(f"{name}_{n}", shape, dt, stack=st)
        sem = lambda n: core.sem(f"{name}_{n}")
        bank_s = [core.ps(f"{name}_ps_scores{k}", st) for k in range(2)]
        bank_j = [core.ps(f"{name}_ps_project{k}", st) for k in range(2)]
        bank_o = [core.ps(f"{name}_ps_context{k}", st) for k in range(2)]
        bank_t = core.ps(f"{name}_ps_tail", st)
        bank_x = core.ps(f"{name}_ps_x", st)
        wq = sb("wq", [128, H * HD])
        wk = sb("wk", [128, H * HD])
        wv = sb("wv", [128, H * HD])
        wo = sb("wo", [128, CH, D])
        bias = sb("bias", [128, D])
        mask = sb("mask", [128, 2, 32])
        quad = sb("quad", [128, 4])
        level_w = sb("level_w", [128, 4])
        xs = sb("xs", [128, D])
        xe = sb("xe", [128, QX + S + KX])
        pairs = sb("pairs", [128, 64])
        quads = sb("quads", [128, 32])
        qT = sb("qT", [128, 2, CH, QW])
        kT = sb("kT", [128, 2, CH, KW])
        val = sb("val", [128, 2, H, VW])
        shifted = sb("shifted", [128, 2, 16, 32])
        top = sb("top", [128, 2, 16])
        probs = sb("probs", [128, 2, 16, 32])
        fine = sb("fine", [128, 2, 8, 32])
        fineT = sb("fineT", [128, 2, 8, 32])
        probsT = sb("probsT", [128, 2, 8, S])
        sums = sb("sums", [128, HG, 4])
        inv = sb("inv", [128, HG])
        ctx = sb("ctx", [128, 2, H, HD])
        ctxT = sb("ctxT", [128, CH, S])
        tail = Tail(core, st, name, bias[:, :])
        tail.bank = bank_x
        s_w = sem("weights_loaded")
        s_set = sem("constants_set")
        s_xs = sem("x_copied")
        s_in = sem("x_in_turned")
        s_xe = sem("x_in_moved")
        s_pool = sem("pool_step")
        s_prj = [sem("projected0"), sem("projected1")]
        s_mov = [sem("moved0"), sem("moved1")]
        s_scores = sem("scores_ready")
        s_sh = sem("shift_step")
        s_shift = sem("shifted")
        s_exp = sem("exp_ready")
        s_fine = sem("expanded")
        s_fineT = sem("expanded_turned")
        s_placed = sem("far_placed")
        s_near = sem("near_placed")
        s_ctx = sem("context_ready")
        s_sum = sem("sum_step")
        s_norm = sem("context_scaled")
        s_cT = sem("context_turned")
        s_cTm = sem("contextT_ready")
        wl = [(wq[:, :], dram["a1_wq"]), (wk[:, :], dram["a1_wk"]), (wv[:, :], dram["a1_wv"]),
              (wo[:, :, :], dram["a1_wo"].rearrange("(c p) n -> p c n", p=128)),
              (bias[:, :], broadcast_rows(dram["a1_bo"], 128)),
              (mask[:, :, :].rearrange("p a n -> p (a n)"), dram["level_mask"]),
              (quad[:, :], dram["quadrant"]), (level_w[:, :], dram["level_weight"])]

        def heads(g):
            return [8 * (g // 2) + 2 * i + g % 2 for i in range(HG)]

        def empty_bank(copy, par, f):
            bank = bank_j[f % 2]
            if f < 8:
                t, n = (qT, QW) if f < 4 else (kT, KW)
                c = 2 * (f % 4)
                return copy(t[:, par, c:c + 2, :].rearrange("p c n -> p (c n)"), bank[:, 0:2 * n])
            h0 = 8 * (f - 8)
            return copy(val[:, par, h0:h0 + 8, 0:HD], bank[:, :].rearrange("p (h d) -> p h d", d=HD))

        with nc.Block() as block:
            @block.sync
            def _(sp):
                for t, source in wl:
                    sp.dma_start(t, source).then_inc(s_w, 16)

            @block.tensor
            def _(pe):
                def turn_in(b):
                    pe.wait_ge(s_xs, b + 1)
                    pe.transpose(bank_x[:, 0:S], xs[:, :], core.ident[:, :]).then_inc(s_in, 1)

                def scores(b, par, X):
                    r = 64 * X
                    for c in range(CH):
                        for j in range(4):
                            p = 32 * j
                            pe.matmul(bank_s[X][p:p + 32, 32 * c:32 * c + 32],
                                      qT[r:r + 64, par, c, QX + p:QX + p + 32],
                                      kT[r:r + 64, par, c, p:p + 32], start=True, stop=True)
                        for j in range(3):
                            p = 32 * j
                            q0 = 32 if j == 2 else 0
                            k0 = S + 32 * j
                            mm = pe.matmul(bank_s[X][p:p + 32, 256 + 32 * c:288 + 32 * c],
                                           qT[r:r + 64, par, c, q0:q0 + 32],
                                           kT[r:r + 64, par, c, k0:k0 + 32], start=True, stop=True)
                    mm.then_inc(s_scores, 1)

                def project(b, par, fills):
                    if 0 in fills:
                        pe.wait_ge(s_pool, 4 * (b + 1))
                    for f in fills:
                        k = f % 2
                        if not (isinstance(b, int) and b == 0 and f < 2):
                            pe.wait_ge(s_mov[k], 5 * b + f // 2)
                        if f < 8:
                            w, n, a = (wq, QW, 0) if f < 4 else (wk, KW, QX)
                            for cc in range(2):
                                c = 2 * (f % 4) + cc
                                mm = pe.matmul(bank_j[k][:, cc * n:(cc + 1) * n], w[:, c * 128:(c + 1) * 128],
                                               xe[:, a:a + n], start=True, stop=True)
                        else:
                            mm = pe.matmul(bank_j[k][:, :], xe[:, QX:QX + S],
                                           wv[:, (f - 8) * 512:(f - 7) * 512], start=True, stop=True)
                        mm.then_inc(s_prj[k], 1)

                def weigh_values(b, par, g):
                    X = g % 2
                    pe.wait_ge(s_near, 2 * b + X + 1)
                    pe.wait_ge(s_placed, 2 * b + X + 1)
                    if not (isinstance(b, int) and b == 0 and g < 2):
                        pe.wait_ge(s_norm, G * b + g - 1)
                    for i, h in enumerate(heads(g)):
                        mm = pe.matmul(bank_o[X][:, i * VW:(i + 1) * VW], probsT[:, X, h // 2, :],
                                       val[:, par, h, :], start=True, stop=True)
                    mm.then_inc(s_ctx, 1)

                def turn_context(b, par, half, wait):
                    pe.wait_ge(s_norm, G * b + 2 * half + 2)
                    if half == 0 and wait:
                        pe.wait_ge(tail.res_step, TAIL_STEPS * b - TAIL_STEPS + 1)
                    if half == 1:
                        pe.wait_ge(s_cTm, 2 * b + 1)
                    for c in range(4 * half, 4 * half + 4):
                        mm = pe.transpose(bank_t[:, (c % 4) * S:(c % 4 + 1) * S],
                                          ctx[:, par, :, :].rearrange("p h d -> p (h d)")
                                          [:, c * 128:(c + 1) * 128], core.ident[:, :])
                    mm.then_inc(s_cT, 1)

                def project_out(b):
                    pe.wait_ge(s_cTm, 2 * (b + 1))
                    for c in range(CH):
                        mm = pe.matmul(bank_t[:, 0:D], ctxT[:, c, :], wo[:, c, :], start=(c == 0),
                                       stop=(c == CH - 1))
                    mm.then_inc(tail.out_ready, 1)

                def batch(b, par, back, more):
                    for k in range(2):
                        pe.wait_ge(s_mov[k], 5 * (b + 1))
                    if more:
                        turn_in(b + 1)
                    scores(b, par, 0)
                    scores(b, par, 1)
                    if back:
                        for g in range(G):
                            weigh_values(b - 1, 1 - par, g)
                    if more:
                        project(b + 1, 1 - par, (0, 1))
                    if back == 2:
                        if more:
                            pe.wait_ge(s_xe, b + 2)
                        tail.turn_x(pe, b - 2, par, bank_x)
                    if back:
                        turn_context(b - 1, 1 - par, 0, back == 2)
                    if more:
                        project(b + 1, 1 - par, (2, 3, 4))
                    if back:
                        turn_context(b - 1, 1 - par, 1, True)
                    if more:
                        project(b + 1, 1 - par, (5, 6, 7))
                    if back:
                        project_out(b - 1)
                    if more:
                        project(b + 1, 1 - par, (8, 9))

                def drain():
                    b = NB - 1
                    for g in range(G):
                        weigh_values(b, 1, g)
                    pe.wait_ge(tail.x_moved, b - 1)
                    tail.turn_x(pe, b - 1, 0, bank_x)
                    turn_context(b, 1, 0, True)
                    turn_context(b, 1, 1, True)
                    project_out(b)
                    pe.wait_ge(tail.x_moved, b)
                    tail.turn_x(pe, b, 1, bank_x)

                pe.wait_ge(s_w, 16 * len(wl))
                pe.wait_ge(s_set, 6)
                turn_in(0)
                project(0, 0, range(FILLS))
                in_pairs(pe, batch, drain)

            @block.scalar
            def _(act):
                def move_in(b):
                    act.wait_ge(s_in, b + 1)
                    act.activation(xe[:, QX:QX + S], bank_x[:, 0:S], ACT.Copy).then_inc(s_xe, 1)

                def exponentials(b, X):
                    act.wait_ge(s_shift, 2 * b + X + 1)
                    act.activation(probs[:, X, :, :].rearrange("p h n -> p (h n)"),
                                   shifted[:, X, :, :].rearrange("p h n -> p (h n)"), ACT.Exp,
                                   scale=float(HD) ** -0.5).then_inc(s_exp, 1)

                def empty(b, par, fills):
                    for f in fills:
                        act.wait_ge(s_prj[f % 2], 5 * b + f // 2 + 1)
                        empty_bank(lambda o, i: act.activation(o, i, ACT.Copy), par, f)\
                            .then_inc(s_mov[f % 2], 1)

                def move_context(b, half):
                    act.wait_ge(s_cT, 2 * b + half + 1)
                    act.activation(ctxT[:, 4 * half:4 * half + 4, :].rearrange("p c n -> p (c n)"),
                                   bank_t[:, :], ACT.Copy).then_inc(s_cTm, 1)

                def batch(b, par, back, more):
                    if more:
                        move_in(b + 1)
                    exponentials(b, 0)
                    exponentials(b, 1)
                    if more:
                        empty(b + 1, 1 - par, (0, 1))
                    if back == 2:
                        tail.move_xT(act, b - 2, bank_x)
                    if back:
                        move_context(b - 1, 0)
                    if more:
                        empty(b + 1, 1 - par, (2, 3, 4))
                    if back:
                        move_context(b - 1, 1)
                    if more:
                        empty(b + 1, 1 - par, range(5, FILLS))

                def drain():
                    b = NB - 1
                    tail.move_xT(act, b - 1, bank_x)
                    move_context(b, 0)
                    move_context(b, 1)
                    tail.move_xT(act, b, bank_x)

                act.wait_ge(s_set, 6)
                move_in(0)
                empty(0, 0, range(FILLS))
                in_pairs(act, batch, drain)

            @block.vector
            def _(v):
                def shift(b, X):
                    n = 2 * b + X
                    sc = shifted[:, X, :, :].rearrange("p (l h) n -> p l h n", l=2)
                    v.wait_ge(s_scores, n + 1)
                    v.tensor_tensor(sc, bank_s[X][:, :].rearrange("p (l h n) -> p l h n", l=2, h=8),
                                    mask[:, :, :].rearrange("p l (h n) -> p l h n", h=1)
                                    .broadcast_to([128, 2, 8, 32]), ALU.add).then_inc(s_sh, 1)
                    v.wait_ge(s_sh, 2 * n + 1)
                    v.tensor_reduce(top[:, X, :], shifted[:, X, :, :], AX.X, ALU.max).then_inc(s_sh, 1)
                    v.wait_ge(s_sh, 2 * n + 2)
                    v.tensor_tensor(shifted[:, X, :, :], shifted[:, X, :, :],
                                    top[:, X, :].rearrange("p (h a) -> p h a", a=1)
                                    .broadcast_to([128, 16, 32]), ALU.subtract).then_inc(s_shift, 1)

                def spread(b, X):
                    n = 2 * b + X
                    v.wait_ge(s_exp, n + 1)
                    near = probs[0:96, X, 8:16, 0:16].rearrange("p h (m a) -> p h m a", a=1)
                    v.tensor_copy(fine[0:96, X, :, :].rearrange("p h (m a) -> p h m a", a=2),
                                  near.broadcast_to([96, 8, 16, 2])).then_inc(s_fine, 1)
                    for j in range(4):
                        p = 32 * j
                        v.transpose(probsT[p:p + 32, X, :, p:p + 32], probs[p:p + 32, X, 0:8, :])
                    v.wait_ge(s_fine, 2 * n + 1)
                    far = probs[0:96, X, 8:16, 16:24].rearrange("p h (m a) -> p h m a", a=1)
                    f4 = fine[0:96, X, :, :].rearrange("p h (m a) -> p h m a", a=4)
                    v.tensor_tensor(f4, f4, far.broadcast_to([96, 8, 8, 4]), ALU.add).then_inc(s_fine, 1)
                    v.wait_ge(s_fine, 2 * n + 2)
                    v.transpose(fineT[0:96, X, :, :], fine[0:96, X, :, :]).then_inc(s_fineT, 1)
                    v.wait_ge(s_fineT, n + 1)
                    v.tensor_copy(probsT[64:96, X, :, 97:128:2], fineT[64:96, X, :, 0:16])\
                        .then_inc(s_near, 1)

                def scale_context(b, par, g):
                    t = G * b + g
                    o3 = bank_o[g % 2][:, 0:HG * VW].rearrange("p (h d) -> p h d", d=VW)
                    v.wait_ge(s_ctx, t + 1)
                    v.tensor_tensor(sums[:, :, :], o3[:, :, HD:VW],
                                    level_w[:, :].rearrange("p (a q) -> p a q", a=1)
                                    .broadcast_to([128, HG, 4]), ALU.mult).then_inc(s_sum, 1)
                    v.wait_ge(s_sum, 4 * t + 1)
                    v.tensor_reduce(inv[:, :], sums[:, :, :], AX.X, ALU.add).then_inc(s_sum, 1)
                    v.wait_ge(s_sum, 4 * t + 2)
                    v.tensor_scalar(inv[:, :], inv[:, :], 1e-8, None, ALU.add).then_inc(s_sum, 1)
                    v.wait_ge(s_sum, 4 * t + 3)
                    v.reciprocal(inv[:, :], inv[:, :]).then_inc(s_sum, 1)
                    v.wait_ge(s_sum, 4 * t + 4)
                    h0 = heads(g)[0]
                    v.tensor_tensor(ctx[:, par, h0:h0 + 7:2, :], o3[:, :, 0:HD],
                                    inv[:, :].rearrange("p (h a) -> p h a", a=1)
                                    .broadcast_to([128, HG, HD]), ALU.mult).then_inc(s_norm, 1)

                def batch(b, par, back, more):
                    shift(b, 0)
                    shift(b, 1)
                    if back == 2:
                        tail.normalise(v, b - 2, par)
                    if back:
                        for g in range(G):
                            scale_context(b - 1, 1 - par, g)
                    spread(b, 0)
                    spread(b, 1)
                    if back:
                        tail.residual(v, b - 1, bank_t[:, 0:D], core.x_all[:, bass.ts(b - 1, D)])

                def drain():
                    b = NB - 1
                    tail.normalise(v, b - 1, 0)
                    for g in range(G):
                        scale_context(b, 1, g)
                    tail.residual(v, b, bank_t[:, 0:D], core.x_all[:, bass.ts(b, D)])
                    tail.normalise(v, b, 1)

                v.wait_ge(s_w, 16 * len(wl))
                v.memset(probsT[:, :, :, :], 0.0).then_inc(s_set, 1)
                for X in range(2):
                    v.memset(bank_s[X][96:128, 256:512], 0.0).then_inc(s_set, 1)
                for par in range(2):
                    v.tensor_copy(val[:, par, :, HD:VW], quad[:, :].rearrange("p (a q) -> p a q", a=1)
                                  .broadcast_to([128, H, 4])).then_inc(s_set, 1)
                v.memset(fine[:, :, :, :], 0.0).then_inc(s_set, 1)
                v.wait_ge(s_set, 6)
                in_pairs(v, batch, drain)

            @block.gpsimd
            def _(pool):
                def copy_in(b):
                    pool.tensor_copy(xs[:, :], core.x_all[:, bass.ts(b, D)]).then_inc(s_xs, 1)

                def half(n):
                    return core.half[:, :].broadcast_to([128, n])

                def pool_x(b):
                    x = xe[:, QX:QX + S]
                    pool.wait_ge(s_xe, b + 1)
                    pool.tensor_tensor(pairs[:, :], x[:, 0:S:2], x[:, 1:S:2], ALU.add).then_inc(s_pool, 1)
                    pool.wait_ge(s_pool, 4 * b + 1)
                    pool.tensor_tensor(pairs[:, :], pairs[:, :], half(64), ALU.mult).then_inc(s_pool, 1)
                    pool.wait_ge(s_pool, 4 * b + 2)
                    pool.tensor_tensor(quads[:, :], pairs[:, 0:64:2], pairs[:, 1:64:2], ALU.add)\
                        .then_inc(s_pool, 1)
                    pool.wait_ge(s_pool, 4 * b + 3)
                    k0 = QX + S
                    for a, q0, n in ((16, 16, 16), (48, 16, 16), (k0 + 16, 0, 16), (k0 + 48, 8, 8),
                                     (k0 + 56, 0, 8), (k0 + 80, 0, 16)):
                        pool.tensor_tensor(xe[:, a:a + n], quads[:, q0:q0 + n], half(n), ALU.mult)
                    for a, p0 in ((0, 16), (32, 48), (k0, 0), (k0 + 32, 0), (k0 + 64, 32)):
                        ins = pool.tensor_copy(xe[:, a:a + 16], pairs[:, p0:p0 + 16])
                    ins.then_inc(s_pool, 1)

                def place(b, X):
                    pool.wait_ge(s_fineT, 2 * b + X + 1)
                    pool.tensor_tensor(probsT[0:32, X, :, 33:64:2], fineT[0:32, X, :, 0:16],
                                       core.zeros[0:32, :].rearrange("p (a n) -> p a n", a=1)
                                       .broadcast_to([32, 8, 16]), ALU.add)
                    pool.tensor_copy(probsT[0:64, X, :, 67:128:4], fineT[0:64, X, :, 16:32])\
                        .then_inc(s_placed, 1)

                def batch(b, par, back, more):
                    if more:
                        pool_x(b + 1)
                        if not (isinstance(b, int) and b == NB - 2):
                            copy_in(b + 2)
                    if back == 2:
                        tail.keep(pool, b - 2, par)
                        tail.keep_T(pool, b - 2)
                    place(b, 0)
                    place(b, 1)
                    if back:
                        tail.rsqrt(pool, b - 1)

                def drain():
                    b = NB - 1
                    tail.keep(pool, b - 1, 0)
                    tail.keep_T(pool, b - 1)
                    tail.rsqrt(pool, b)
                    tail.keep(pool, b, 1)
                    tail.keep_T(pool, b)

                tail.open_xT(pool)
                copy_in(0)
                pool_x(0)
                copy_in(1)
                in_pairs(pool, batch, drain)


def decoder_kernel(nc, dram, out, emb):
    stack = ExitStack()
    with stack:
        core = Core(nc, stack, dram)
        setup_phase(core)
        core.end_phase()
        attention_phase(core, "l0a", "rope", 8, float(8) ** -0.5, True, None, "a0")
        core.end_phase()
        attention_phase(core, "l0x", "cross", 64, float(64) ** -0.5, False, "f0_router", "x0")
        core.end_phase()
        expert_phase(core, "l0f", False, None)
        core.end_phase()
        block_attention_phase(core)
        core.end_phase()
        geometry_phase(core, emb)
        core.end_phase()
        attention_phase(core, "l1x", "boxes", 64, float(64) ** -0.5, True, "f1_router", "x1", emb)
        core.end_phase()
        expert_phase(core, "l1f", True, out)


def constants():
    f = np.float32
    c = {"identity": np.eye(128, dtype=f)}
    inv_freq = (f(1.0) / f(10000.0) ** (np.arange(0, 8, 2, dtype=f) / f(8))).astype(f)
    ang = (np.arange(S, dtype=f)[:, None] * inv_freq[None, :]).astype(f)
    cos, sin = np.cos(ang).astype(f), np.sin(ang).astype(f)
    c["rope_cos"] = np.concatenate([cos, cos], 1)
    c["rope_sin"] = np.concatenate([-sin, sin], 1)
    c["order"] = np.arange(E, 0, -1).astype(f)
    r = np.arange(32)
    near = (r[:, None] // 16 == r[None, :] // 16) & (r[None, :] <= r[:, None])
    far = r[:, None] // 16 == r[None, :] // 16
    m = np.where(np.concatenate([near, far], 1), 0.0, NEG).astype(f)
    c["level_mask"] = np.tile(m, (4, 1))
    q = np.arange(128) // 32
    c["quadrant"] = (q[:, None] == np.arange(4)[None, :]).astype(f)
    lw = np.array([[1, 0, 0, 0], [.5, 1, 0, 0], [.25, .25, 1, 0], [.25, .25, .5, 1]], dtype=f)
    c["level_weight"] = lw[q]
    return c


def host_arrays(x, ctx_1024, fside_BxSx4_0, **w):
    a = {k: np.asarray(v) for k, v in w.items()}
    x, ctx, box = np.asarray(x), np.asarray(ctx_1024), np.asarray(fside_BxSx4_0)
    c = {"x": x, "xT": x.transpose(0, 2, 1), "ctxT": ctx.transpose(0, 2, 1)}
    boxT = box.transpose(0, 2, 1)
    c["boxesT"] = boxT
    for side, key in ((0, "boxes_lo_j"), (1, "boxes_hi_j")):
        t = boxT[:, 2 * side:2 * side + 2, :].reshape(NB // 2, 2, 2, 8, 16)
        t = t.transpose(1, 2, 4, 0, 3).reshape(64, NB // 2 * 8)
        c[key] = np.concatenate([t, t], 0)
    c["a0_wqkv"] = np.concatenate([a["L0_attn_Wq"].T, a["L0_attn_Wk"].T, a["L0_attn_Wv"].T], 1)
    c["a0_bqkv"] = np.concatenate([a["L0_attn_bq"], a["L0_attn_bk"], a["L0_attn_bv"]])
    c["a0_wo"] = a["L0_attn_Wo"].T
    c["a0_bo"] = a["L0_attn_bo"]
    for k in ("q", "k", "v", "o"):
        c["x0_w" + k] = a["L0_xattn_W" + k]
        c["x1_w" + k] = a["L1_xattn_W" + k].T
    qkv = a["L1_attn_w_qkv"]
    for i, k in enumerate("qkv"):
        c["a1_w" + k] = qkv[i * 1024:(i + 1) * 1024].T
    c["a1_wo"] = a["L1_attn_w_out"].T
    c["a1_bo"] = a["L1_attn_b_out"]
    for k in ("q", "k", "v"):
        c["x1_b" + k] = a["L1_xattn_b" + k].reshape(8, 128).T
    c["x1_bo"] = a["L1_xattn_bo"]
    c["x1_bg"] = a["L1_xattn_bg"]
    wg = a["L1_xattn_Wg"]
    sel = np.zeros((8, 16, H, 16), np.float32)
    for j in range(16):
        sel[:, j, :, j] = wg.T
    c["x1_wbox_sel"] = sel.reshape(128, H * 16)
    for p, n in (("f0", "L0_ffn_"), ("f1", "L1_ffn_")):
        r = "switch_" if p == "f0" else "router_"
        c[p + "_router_w"], c[p + "_router_b"] = a[n + r + "w"], a[n + r + "b"]
        c[p + "_w1"], c[p + "_w2"], c[p + "_b2"] = a[n + "w1"], a[n + "w2"], a[n + "b2"]
        c[p + "_b1"] = a[n + "b1"].reshape(E, FC, 128).transpose(2, 0, 1).reshape(128, E * FC)
    c.update(constants())
    return {k: np.ascontiguousarray(v) for k, v in c.items()}


def kernel(**inputs):
    import concourse.bacc as bacc
    from concourse.bass_utils import run_bass_kernel_spmd

    nc = bacc.Bacc("TRN2", target_bir_lowering=False, num_devices=1)
    arrays = {"in_" + k: v for k, v in host_arrays(**inputs).items()}
    dram = {k[3:]: nc.dram_tensor(k, v.shape, mybir.dt.from_np(v.dtype), kind="ExternalInput").ap()
            for k, v in arrays.items()}
    out = nc.dram_tensor("out_x", (NB, S, D), F32, kind="ExternalOutput").ap()
    emb = nc.dram_tensor("box_features", (NB // 2, 2, 128, 8 * S), F32, kind="Internal").ap()
    decoder_kernel(nc, dram, out, emb)
    r = run_bass_kernel_spmd(nc, [arrays], core_ids=[0])
    return r.results[0]["out_x"]
```

```python
from contextlib import ExitStack

import numpy as np

import concourse.bass as bass
from concourse import mybir

F32 = mybir.dt.float32
BF16 = mybir.dt.bfloat16
F32R = mybir.dt.float32r
ALU = mybir.AluOpType
ACT = mybir.ActivationFunctionType
AX = mybir.AxisListType

NB = 32
S = 128
D = 128
H = 16
G = 4
HG = H // G
E = 8
F = 512
FC = F // 128
TB = 512
NT = NB * S // TB
TT = TB // S
EPS = 1e-5
CLIP = 1e-6
NEG = -1e30
TWO_PI_HI = 6.28125
TWO_PI_LO = 2 * np.pi - 6.28125
MAGIC = 1.5 * 2.0 ** 23
ANGLE_MAX = 3.1415925


class Core:

    def __init__(self, nc, stack, dram):
        self.nc = nc
        self.stack = stack
        self.dram = dram
        self.sems = []
        self.started = nc.alloc_semaphore("started")
        self.x_all = self.sb("x_all", [128, NB * D])
        self.xT_all = self.sb("xT_all", [128, NB * S])
        self.logits_all = self.sb("logits_all", [128, NB * E])
        self.ident = self.sb("ident", [128, 128])
        self.half_power = self.sb("half_power", [128, 4])
        self.eps_tile = self.sb("eps_tile", [128, 4])
        self.zeros = self.sb("zeros", [128, 1])
        self.half = self.sb("half", [128, 1])
        self.dve_mark = self.sb("dve_mark", [128, 1])
        self.att_w = [self.sb(f"att_w{n}", [128, H * 64]) for n in "qkv"]
        self.att_wo = self.sb("att_wo", [128, H * 64 // 128, D])
        self.att_loaded = nc.alloc_semaphore("att_weights_loaded")
        self.hid = self.sb("hidden", [128, 2, FC, TB])
        self.w1 = self.hid[:, :, :, :].rearrange("p a c n -> p (a c n)").rearrange("p (e f) -> p e f", e=E)
        self.w2 = self.sb("experts_w2", [128, E, FC, D])
        self.experts_loaded = nc.alloc_semaphore("experts_loaded")

    def sb(self, name, shape, dt=F32, stack=None):
        return (stack or self.stack).enter_context(self.nc.sbuf_tensor(name, shape, dt))

    def ps(self, name, stack, shape=(128, 512), dt=F32):
        return stack.enter_context(self.nc.psum_tensor(name, list(shape), dt))

    def sem(self, name):
        handle = self.nc.alloc_semaphore(name)
        self.sems.append(handle)
        return handle

    def wait_apart(self, v, sem, value):
        v.wait_ge(sem, value)
        v.tensor_copy(self.dve_mark[:, :], self.eps_tile[:, 0:1])

    def load_attention(self, sp, weights):
        for t, n in zip(self.att_w, "qkv"):
            sp.dma_start(t[:, :], self.dram[f"{weights}_w{n}"]).then_inc(self.att_loaded, 16)
        sp.dma_start(self.att_wo[:, :, :], self.dram[weights + "_wo"].rearrange("(c p) n -> p c n", p=128))\
            .then_inc(self.att_loaded, 16)

    def load_experts(self, sp, weights):
        for e in range(E):
            sp.dma_start(self.w1[:, e, :], self.dram[weights + "_w1"][e]).then_inc(self.experts_loaded, 16)
            sp.dma_start(self.w2[:, e, :, :],
                         self.dram[weights + "_w2"][e].rearrange("(c p) n -> p c n", p=128))\
                .then_inc(self.experts_loaded, 16)

    def end_phase(self):
        self.nc.clear_and_free_semaphores(self.sems)
        self.nc.all_engine_barrier()
        self.sems = []


def loads(n, b, par):
    return 8 * n * (b - par + 2)


def in_pairs(eng, batch, drain):
    batch(0, 0, 0, True)
    batch(1, 1, 1, True)
    with eng.Fori(0, NB // 2 - 2) as i:
        first = 2 * i + 2
        batch(first, 0, 2, True)
        batch(first + 1, 1, 2, True)
    batch(NB - 2, 0, 2, True)
    batch(NB - 1, 1, 2, False)
    drain()


def first_apart(eng, n, step, apart=1, last=0):
    for i in range(apart):
        step(i)
    with eng.Fori(apart, n - last) as i:
        step(i)
    for i in range(n - last, n):
        step(i)


def is_first(i):
    return isinstance(i, int) and i == 0


def broadcast_rows(ap, n):
    return bass.AP(tensor=ap.tensor, offset=ap.offset, ap=[[0, n]] + [list(p) for p in ap.ap])


def setup_phase(core):
    nc = core.nc
    s_consts = core.sem("consts_loaded")
    with nc.Block() as block:
        @block.sync
        def _(sp):
            sp.dma_start(core.ident[:, :], core.dram["identity"]).then_inc(s_consts, 16)
            sp.wait_ge(s_consts, 16)

        @block.gpsimd
        def _(pool):
            pool.memset(core.half_power[:, :], -0.5)
            pool.memset(core.zeros[:, :], 0.0)
            pool.memset(core.half[:, :], 0.5)
            pool.memset(core.eps_tile[:, :], EPS).then_inc(core.started, 1)
            pool.wait_ge(core.started, 1)


class Geometry:
    NJ = 8
    PB = NB // 2
    K = 64

    def __init__(self, core, st, emb):
        sb = lambda n, shape: core.sb("geo_" + n, shape, stack=st)
        NJ, PB = self.NJ, self.PB
        W = self.W = 2 * NJ * S
        self.dram, self.emb = core.dram, emb
        self.lo = sb("lo", [128, PB * S])
        self.hi = sb("hi", [128, PB * S])
        self.size = sb("size", [128, PB * S])
        self.lo_j = sb("lo_j", [128, PB * NJ])
        self.hi_j = sb("hi_j", [128, PB * NJ])
        self.size_j = sb("size_j", [128, PB * NJ])
        self.magic = sb("magic", [128, 2])
        self.quarter = sb("quarter", [128, 1])
        self.pos = sb("pos", [128, W])
        self.turns = sb("turns", [128, W])
        self.feat = sb("feat", [128, 2, W])
        self.s_in = core.sem("geo_boxes_loaded")
        self.s_pre = core.sem("geo_prepared")
        self.s_prelog = core.sem("geo_log_sizes")
        self.s_d = core.sem("geo_distance_step")
        self.s_dist = core.sem("geo_distance_ready")
        self.s_a = core.sem("geo_log_step")
        self.s_turns = core.sem("geo_turns_ready")
        self.s_r = core.sem("geo_reduce_step")
        self.s_angle = core.sem("geo_angle_ready")
        self.s_abs = core.sem("geo_abs_ready")
        self.s_feat = core.sem("geo_features_ready")
        self.s_out = core.sem("geo_stored")

    def load(self, sp):
        boxes = self.dram["boxesT"].rearrange("(i a) c n -> a c i n", a=2)
        for kind in range(2):
            for a in range(2):
                for co in range(2):
                    p = 64 * kind + 32 * a + 16 * co
                    for t, side in ((self.lo, 0), (self.hi, 1)):
                        sp.dma_start(t[p:p + 16, :].rearrange("p (b n) -> p b n", b=self.PB),
                                     broadcast_rows(boxes[a, 2 * side + co], 16)).then_inc(self.s_in, 16)
        sp.dma_start(self.lo_j[:, :], self.dram["boxes_lo_j"]).then_inc(self.s_in, 16)
        sp.dma_start(self.hi_j[:, :], self.dram["boxes_hi_j"]).then_inc(self.s_in, 16)

    def store(self, sp):
        with sp.Fori(0, NT) as q:
            sp.wait_ge(self.s_feat, q + 1)
            for c in range(2):
                for trig in range(2):
                    sp.dma_start(self.emb[bass.ds(2 * q + c, 1), trig, :, :].rearrange("a p n -> p (a n)"),
                                 self.feat[:, trig, c * self.NJ * S:(c + 1) * self.NJ * S])\
                        .then_inc(self.s_out, 16)
        sp.wait_ge(self.s_out, 64 * NT)

    def sizes(self, v):
        v.wait_ge(self.s_in, 16 * 18)
        v.memset(self.magic[:, 0:1], MAGIC)
        v.memset(self.magic[:, 1:2], -MAGIC)
        v.memset(self.quarter[:, :], float(np.pi / 2))
        v.tensor_tensor(self.size[:, :], self.hi[:, :], self.lo[:, :], ALU.subtract)
        v.tensor_tensor(self.size_j[:, :], self.hi_j[:, :], self.lo_j[:, :], ALU.subtract)\
            .then_inc(self.s_pre, 1)
        v.wait_ge(self.s_pre, 1)
        v.tensor_scalar(self.size[:, :], self.size[:, :], 1.0, None, ALU.add)
        v.tensor_scalar(self.size_j[:, :], self.size_j[:, :], 1.0, None, ALU.add).then_inc(self.s_pre, 1)

    def centres(self, v):
        K, lo, hi, lo_j, hi_j = self.K, self.lo, self.hi, self.lo_j, self.hi_j
        v.tensor_tensor(lo[0:K, :], lo[0:K, :], hi[0:K, :], ALU.add)
        v.tensor_tensor(lo_j[0:K, :], lo_j[0:K, :], hi_j[0:K, :], ALU.add).then_inc(self.s_pre, 1)
        v.wait_ge(self.s_pre, 3)
        v.tensor_scalar(lo[0:K, :], lo[0:K, :], 0.5, None, ALU.mult)
        v.tensor_scalar(lo_j[0:K, :], lo_j[0:K, :], 0.5, None, ALU.mult)
        v.reciprocal(self.size[0:K, :], self.size[0:K, :]).then_inc(self.s_pre, 1)

    def log_sizes(self, act):
        K = self.K
        act.wait_ge(self.s_pre, 2)
        act.activation(self.lo[K:128, :], self.size[K:128, :], ACT.Ln).then_inc(self.s_prelog, 1)
        act.activation(self.lo_j[K:128, :], self.size_j[K:128, :], ACT.Ln).then_inc(self.s_prelog, 1)

    def grid(self, t, q, rows):
        return t[0:rows, bass.ts(q, 2 * S)].rearrange("p (c a n) -> p c a n", c=2, a=1)\
            .broadcast_to([rows, 2, self.NJ, S])

    def distance(self, v, q):
        NJ, K = self.NJ, self.K
        t = self.pos[:, :].rearrange("p (c n m) -> p c n m", c=2, n=NJ)
        if isinstance(q, int) and q == 0:
            v.wait_ge(self.s_prelog, 2)
            v.wait_ge(self.s_pre, 4)
        else:
            v.wait_ge(self.s_feat, q)
        cols = self.lo_j[:, bass.ts(q, 2 * NJ)].rearrange("p (c n a) -> p c n a", c=2, a=1)\
            .broadcast_to([128, 2, NJ, S])
        v.tensor_tensor(t, self.grid(self.lo, q, 128), cols, ALU.subtract).then_inc(self.s_d, 1)
        v.wait_ge(self.s_d, 3 * q + 1)
        v.tensor_tensor(t[0:K], t[0:K], self.grid(self.size, q, K), ALU.mult).then_inc(self.s_d, 1)

    def floor(self, v, q):
        t = self.pos[0:self.K, :]
        v.wait_ge(self.s_d, 3 * q + 2)
        v.scalar_tensor_tensor(out=t, in0=t, scalar=-1.0, in1=t, op0=ALU.mult, op1=ALU.max)\
            .then_inc(self.s_d, 1)
        v.wait_ge(self.s_d, 3 * q + 3)
        v.tensor_scalar(t, t, 0.001, None, ALU.max).then_inc(self.s_dist, 1)

    def log(self, act, q):
        act.wait_ge(self.s_dist, q + 1)
        act.activation(self.pos[0:self.K, :], self.pos[0:self.K, :], ACT.Ln).then_inc(self.s_a, 1)

    def turn(self, act, q):
        act.wait_ge(self.s_a, 3 * q + 1)
        act.activation(self.pos[:, :], self.pos[:, :], ACT.Copy, scale=100.0).then_inc(self.s_a, 1)
        act.wait_ge(self.s_a, 3 * q + 2)
        act.activation(self.turns[:, :], self.pos[:, :], ACT.Identity, bias=self.magic[:, 0:1],
                       scale=float(1 / (2 * np.pi))).then_inc(self.s_a, 1)

    def whole(self, act, q):
        act.wait_ge(self.s_a, 3 * q + 3)
        act.activation(self.turns[:, :], self.turns[:, :], ACT.Identity, bias=self.magic[:, 1:2])\
            .then_inc(self.s_turns, 1)

    def reduce(self, v, q):
        t, m = self.pos[:, :], self.turns[:, :]
        v.wait_ge(self.s_turns, q + 1)
        v.scalar_tensor_tensor(out=t, in0=m, scalar=-TWO_PI_HI, in1=t, op0=ALU.mult, op1=ALU.add)\
            .then_inc(self.s_r, 1)
        v.wait_ge(self.s_r, 2 * q + 1)
        v.scalar_tensor_tensor(out=t, in0=m, scalar=-TWO_PI_LO, in1=t, op0=ALU.mult, op1=ALU.add)\
            .then_inc(self.s_r, 1)
        v.wait_ge(self.s_r, 2 * q + 2)
        v.tensor_scalar(t, t, ANGLE_MAX, -ANGLE_MAX, ALU.min, ALU.max).then_inc(self.s_angle, 1)

    def sine(self, act, q):
        act.wait_ge(self.s_angle, q + 1)
        if not (isinstance(q, int) and q == 0):
            act.wait_ge(self.s_out, 64 * q)
        act.activation(self.feat[:, 0, :], self.pos[:, :], ACT.Sin)

    def absolute(self, act):
        act.activation(self.pos[:, :], self.pos[:, :], ACT.Abs).then_inc(self.s_abs, 1)

    def cosine(self, act, q):
        act.wait_ge(self.s_abs, q + 1)
        act.activation(self.feat[:, 1, :], self.pos[:, :], ACT.Sin, bias=self.quarter[:, 0:1], scale=-1.0)\
            .then_inc(self.s_feat, 1)

    def beside_act(self, act, i, e):
        first = isinstance(i, int) and i == 0
        if first:
            if e == 2:
                self.log_sizes(act)
        elif e == 0:
            self.whole(act, i - 1)
        elif e == 2:
            self.sine(act, i - 1)
        elif e == 3:
            self.absolute(act)
        elif e == 4:
            self.cosine(act, i - 1)
        if e == 6:
            self.log(act, i)
        elif e == 7:
            self.turn(act, i)

    def beside_dve(self, v, i, e):
        first = isinstance(i, int) and i == 0
        if first and e == 0:
            self.sizes(v)
        elif first and e == 1:
            self.centres(v)
        elif e == 0:
            self.reduce(v, i - 1)
        if e == 3:
            self.distance(v, i)
        elif e == 4:
            self.floor(v, i)

    def last_act(self, act):
        self.whole(act, NT - 1)
        self.sine(act, NT - 1)
        self.absolute(act)
        self.cosine(act, NT - 1)


class Tail:

    def __init__(self, core, st, name, bias, router=None):
        self.core = core
        self.name = name
        self.bias = bias
        self.router = router
        self.res = core.sb(name + "_res", [128, D], stack=st)
        self.stats = core.sb(name + "_stats", [128, 6], stack=st)
        self.mv = core.sb(name + "_mv", [128, 2], stack=st)
        self.vpe = core.sb(name + "_vpe", [128, 1], stack=st)
        self.rstd = core.sb(name + "_rstd", [128, 1], stack=st)
        self.xn = core.sb(name + "_xn", [128, 2, D], stack=st)
        self.xs = core.sb(name + "_xTs", [128, S], stack=st)
        self.out_ready = core.sem(name + "_out_ready")
        self.res_step = core.sem(name + "_res_step")
        self.eps_added = core.sem(name + "_eps_added")
        self.rstd_ready = core.sem(name + "_rstd_ready")
        self.xn_ready = core.sem(name + "_xn_ready")
        self.xn_kept = core.sem(name + "_xn_kept")
        self.x_turned = core.sem(name + "_x_turned")
        self.x_moved = core.sem(name + "_x_moved")
        self.xT_kept = core.sem(name + "_xT_kept")
        self.logits_ready = core.sem(name + "_logits_ready")
        self.logits_moved = core.sem(name + "_logits_moved")

    def residual(self, v, b, y, x_in):
        k = 3 + (self.bias is not None)
        v.wait_ge(self.out_ready, b + 1)
        v.tensor_tensor(self.res[:, :], y, x_in, ALU.add).then_inc(self.res_step, 1)
        v.wait_ge(self.res_step, k * b + 1)
        if self.bias is not None:
            v.tensor_tensor(self.res[:, :], self.res[:, :], self.bias, ALU.add).then_inc(self.res_step, 1)
            v.wait_ge(self.res_step, k * b + 2)
        v.bn_stats(self.stats[:, :], self.res[:, :]).then_inc(self.res_step, 1)
        self.core.wait_apart(v, self.res_step, k * b + k - 1)
        v.bn_aggr(self.mv[:, :], self.stats[:, :]).then_inc(self.res_step, 1)

    def rsqrt(self, pool, b):
        k = 3 + (self.bias is not None)
        pool.wait_ge(self.res_step, k * b + k)
        pool.tensor_tensor(self.vpe[:, :], self.mv[:, 1:2], self.core.eps_tile[:, 0:1], ALU.add)\
            .then_inc(self.eps_added, 1)
        pool.wait_ge(self.eps_added, b + 1)
        pool.tensor_tensor(self.rstd[:, :], self.vpe[:, :], self.core.half_power[:, 0:1], ALU.pow)\
            .then_inc(self.rstd_ready, 1)

    def normalise(self, v, b, par):
        v.wait_ge(self.rstd_ready, b + 1)
        v.tensor_scalar(self.xn[:, par, :], self.res[:, :], self.mv[:, 0:1], self.rstd[:, 0:1],
                        ALU.subtract, ALU.mult).then_inc(self.xn_ready, 1)

    def keep(self, pool, b, par):
        pool.wait_ge(self.xn_ready, b + 1)
        pool.tensor_copy(self.core.x_all[:, bass.ts(b, D)], self.xn[:, par, :]).then_inc(self.xn_kept, 1)

    def turn_x(self, pe, b, par, bank):
        pe.wait_ge(self.xn_ready, b + 1)
        pe.transpose(bank[:, 0:S], self.xn[:, par, :], self.core.ident[:, :]).then_inc(self.x_turned, 1)

    def open_xT(self, pool):
        pool.memset(self.xs[:, :], 0.0).then_inc(self.xT_kept, 1)

    def move_xT(self, act, b, bank):
        act.wait_ge(self.x_turned, b + 1)
        act.wait_ge(self.xT_kept, b + 1)
        act.activation(self.xs[:, :], bank[:, 0:S], ACT.Copy).then_inc(self.x_moved, 1)

    def keep_T(self, pool, b):
        pool.wait_ge(self.x_moved, b + 1)
        pool.tensor_copy(self.core.xT_all[:, bass.ts(b, S)], self.xs[:, :]).then_inc(self.xT_kept, 1)

    def route(self, pe, b, bank):
        if self.router is None:
            return
        pe.wait_ge(self.x_moved, b + 1)
        pe.matmul(bank[:, S:S + E], self.xs[:, :], self.router[0], start=True, stop=True)\
            .then_inc(self.logits_ready, 1)

    def move_logits(self, v, b):
        if self.router is None:
            return
        v.wait_ge(self.logits_ready, b + 1)
        v.tensor_tensor(self.core.logits_all[:, bass.ts(b, E)], self.bank[:, S:S + E], self.router[1],
                        ALU.add).then_inc(self.logits_moved, 1)

    def bank_free(self, pe, b):
        pe.wait_ge(self.x_moved, b + 1)
        if self.router is not None:
            pe.wait_ge(self.logits_moved, b + 1)


def attention_phase(core, name, kind, hd, scale, out_bias, router, weights, ahead, emb=None):
    nc, dram = core.nc, core.dram
    rope, boxes = kind == "rope", kind == "boxes"
    HC = 128 // hd if not rope else 4
    NCH = H // HC
    CH = H * hd // 128
    VW = 32 if rope else hd + 1
    NV = 4 if rope else H
    st = ExitStack()

    def head(g, i):
        return (HG * g + i) if rope else (8 * (g // 2) + 2 * i + g % 2)

    with st:
        sb = lambda n, shape, dt=F32: core.sb(f"{name}_{n}", shape, dt, stack=st)
        sem = lambda n: core.sem(f"{name}_{n}")
        bank_s = [core.ps(f"{name}_ps_scores{k}", st) for k in range(2)]
        bank_p = core.ps(f"{name}_ps_turned", st)
        bank_o = core.ps(f"{name}_ps_context", st)
        bank_j = [core.ps(f"{name}_ps_project{k}", st) for k in range(1 if boxes else 2)]
        bank_j = bank_j * 2 if boxes else bank_j
        bank_t = core.ps(f"{name}_ps_tail", st)
        bank_g = [core.ps(f"{name}_ps_boxes{k}", st) for k in range(2 if boxes else 1)]
        qT = sb("qT", [128, 2, NCH, S])
        kT = sb("kT", [128, 2, 1 if rope else NCH, S])
        val = sb("val", [128, 2, NV, VW])
        shifted = sb("shifted", [128, 2, HG, S])
        probs = sb("probs", [128, G, HG, S])
        probsT = sb("probsT", [128, HG, S])
        top = sb("top", [128, 2, HG])
        inv = sb("inv", [128, HG])
        ctx = sb("ctx", [128, 2, H, hd])
        ctxT = sb("ctxT", [128, CH, S])
        wo = sb("wo", [128, CH, D]) if rope else core.att_wo
        bias = sb("out_bias", [128, D]) if out_bias else None
        rw = sb("router_w", [128, E]) if router else None
        rb = sb("router_b", [128, E]) if router else None
        if rope:
            wqkv = sb("wqkv", [128, 192])
            bqkv = sb("bqkv", [128, 192])
            cos = sb("cos", [128, 8])
            sin = sb("sin", [128, 8])
            z = sb("z", [128, 192])
            zc = sb("zc", [128, 160])
            zs = sb("zs", [128, 160])
            qpad = sb("qpad", [128, H, 32])
            kpad = sb("kpad", [128, 4, 32])
            raw = sb("raw", [128, HG, S])
            inv_all = sb("inv_all", [128, H])
            s_raw = sem("raw_context_moved")
            s_val = sem("values_ready")
            s_back = sem("raw_context_turned")
            src = sb("xT_in", [128, 2, S])
        else:
            wq, wk, wv = core.att_w
            src = sb("cT_in", [128, 2, S])
        if boxes:
            bq = sb("bq", [128, NCH])
            bk = sb("bk", [128, NCH])
            bv = sb("bv", [128, CH])
            bv_wide = sb("bv_wide", [128, CH, 128])
            wbox = sb("wbox", [128, H, 16])
            KB = 96
            bg_rest = sb("bg_rest", [KB, H])
            bg_part = sb("bg_part", [KB, 3, H], BF16)
            bg_wide = sb("bg_wide", [KB, H, 64], BF16)
            ones = sb("ones", [KB, 128], BF16)
            feats = sb("feats", [128, 2, 8, S])
            s_bg = sem("box_bias_step")
            s_feats = [sem(f"feats_loaded{k}") for k in range(2)]
            s_box = sem("box_weights_ready")
            s_gated = sem("gated")
            s_bias = sem("bias_step")
        tail = Tail(core, st, name, bias[:, :] if out_bias else None,
                    (rw[:, :], rb[:, :]) if router else None)
        tail.bank = bank_t
        s_w = sem("weights_loaded")
        s_x = sem("x_loaded")
        s_ones = sem("ones_ready")
        s_src = [sem(f"src_loaded{k}") for k in range(2)]
        s_prj = [sem("projected0"), sem("projected1")]
        s_mov = [sem("moved0"), sem("moved1")]
        s_rope = sem("rope_step")
        s_pad = sem("padded")
        s_scores = sem("scores_ready")
        s_top = sem("top_ready")
        s_shift = sem("shifted")
        s_exp = sem("exp_ready")
        s_turn = sem("probs_turned")
        s_pT = sem("probsT_ready")
        s_ctx = sem("context_ready")
        s_inv = sem("sums_inverted")
        s_norm = sem("context_scaled")
        s_cT = sem("context_turned")
        s_cTm = sem("contextT_ready")

        wl = []
        if rope:
            wl += [(wqkv[:, :], dram["a0_wqkv"]), (bqkv[:, :], broadcast_rows(dram["a0_bqkv"], 128)),
                   (cos[:, :], dram["rope_cos"]), (sin[:, :], dram["rope_sin"]),
                   (wo[:, 0, :], dram["a0_wo"]),
                   (bias[:, :], broadcast_rows(dram["a0_bo"], 128))]
        if boxes:
            wl += [(bq[:, :], dram["x1_bq"]), (bk[:, :], dram["x1_bk"]), (bv[:, :], dram["x1_bv"]),
                   (bias[:, :], broadcast_rows(dram["x1_bo"], 128)),
                   (wbox[:, :, :].rearrange("p h j -> p (h j)"), dram["x1_wbox_sel"]),
                   (bg_rest[:, :], broadcast_rows(dram["x1_bg"], KB))]
        if router:
            wl += [(rw[:, :], dram[router + "_w"]), (rb[:, :], broadcast_rows(dram[router + "_b"], 128))]
        n_w = len(wl)
        HALVES = 1 if rope else 2
        FILLS = [2, 1] if rope else [3, 3]

        with nc.Block() as block:
            @block.sync
            def _(sp):
                for t, source in wl:
                    sp.dma_start(t, source).then_inc(s_w, 16)

                def load(half, par, wait):
                    b = 2 * half + par
                    if wait:
                        sp.wait_ge(s_box if boxes else s_prj[1], (2 if boxes else FILLS[1]) * (b - 1))
                    if rope:
                        sp.dma_start(src[:, par, :], dram["xT"][bass.ds(b, 1), :, :]
                                     .rearrange("a p n -> p (a n)")).then_inc(s_src[par], 16)
                    else:
                        sp.dma_start(src[:, par, :], dram["ctxT"][bass.ds(b, 1), :, :]
                                     .rearrange("a p n -> p (a n)")).then_inc(s_src[par], 16)
                    if boxes:
                        for trig in range(2):
                            for kind in range(2):
                                p, r = 64 * trig + 32 * kind, 64 * kind + 32 * par
                                sp.dma_start(feats[p:p + 32, par, :, :].rearrange("p a n -> p (a n)"),
                                             emb[bass.ds(half, 1), trig, r:r + 32, :]
                                             .rearrange("a p n -> p (a n)")).then_inc(s_feats[par], 16)

                load(0, 0, False)
                load(0, 1, False)
                if rope:
                    sp.dma_start(core.x_all[:, :].rearrange("p (b n) -> p b n", b=NB),
                                 dram["x"].rearrange("b p n -> p b n")).then_inc(s_x, 16)
                ahead(sp)
                with sp.Fori(1, NB // 2) as i:
                    load(i, 0, True)
                    load(i, 1, True)

            @block.tensor
            def _(pe):
                def fill(k, b, n):
                    if boxes:
                        if k == 1:
                            pe.wait_ge(s_mov[0], FILLS[0] * b + n + 1)
                        elif not (isinstance(b, int) and FILLS[1] * b + n == 0):
                            pe.wait_ge(s_mov[1], FILLS[1] * b + n)
                        return
                    if isinstance(b, int) and FILLS[k] * b + n == 0:
                        return
                    pe.wait_ge(s_mov[k], FILLS[k] * b + n)

                def project(b, par, part, banks=(0, 1)):
                    if rope:
                        if part == 0:
                            pe.wait_ge(s_src[par], loads(1, b, par))
                            fill(0, b, 0)
                            pe.matmul(bank_j[0][:, 0:192], src[:, par, :], wqkv[:, :], start=True, stop=True)\
                                .then_inc(s_prj[0], 1)
                        if part == 2:
                            pe.wait_ge(s_pad, b + 1)
                            fill(1, b, 0)
                            for r in range(4):
                                mm = pe.transpose(bank_j[1][:, r * S:(r + 1) * S],
                                                  qpad[:, 4 * r:4 * r + 4, :].rearrange("p h d -> p (h d)"),
                                                  core.ident[:, :])
                            mm.then_inc(s_prj[1], 1)
                            fill(0, b, 1)
                            pe.transpose(bank_j[0][:, 0:S], kpad[:, :, :].rearrange("p h d -> p (h d)"),
                                         core.ident[:, :]).then_inc(s_prj[0], 1)
                        return
                    if part == 0 and 0 in banks:
                        pe.wait_ge(s_src[par], loads(1, b, par))
                    if part == 3:
                        return
                    for k in banks:
                        fill(k, b, part)
                        if part < 2:
                            w = wq if part == 0 else wk
                            xr = core.xT_all[:, bass.ts(b, S)] if part == 0 else src[:, par, :]
                            for cc in range(4):
                                c = 4 * k + cc
                                mm = pe.matmul(bank_j[k][:, cc * S:(cc + 1) * S], w[:, c * 128:(c + 1) * 128],
                                               xr, start=True, stop=True)
                        else:
                            mm = pe.matmul(bank_j[k][:, :], src[:, par, :], wv[:, k * 512:(k + 1) * 512],
                                           start=True, stop=True)
                        mm.then_inc(s_prj[k], 1)

                def scores(b, par, g, first):
                    t = G * b + g
                    pe.wait_ge(s_mov[0], FILLS[0] * (b + 1) - (0 if rope else 1))
                    pe.wait_ge(s_mov[1], FILLS[1] * (b + 1) - (0 if rope else 1))
                    if not (first and g < 2):
                        pe.wait_ge(s_shift, t - 1)
                    for i in range(HG):
                        h = head(g, i)
                        c, r = (i, 32 * g) if rope else (h // HC, 128 // HC * (h % HC))
                        mm = pe.matmul(bank_s[g % 2][:, i * S:(i + 1) * S], qT[r:r + hd, par, c, :],
                                       kT[r:r + hd, par, 0 if rope else c, :], start=True, stop=True)
                    mm.then_inc(s_scores, 1)
                    if boxes and g % 2 == 0:
                        if g == 0:
                            pe.wait_ge(s_feats[par], loads(4, b, par))
                        if not (first and g == 0):
                            pe.wait_ge(s_gated, t)
                        h0 = 8 * (g // 2)
                        for X in range(2):
                            pe.matmul(bank_g[X][:, :], ones[:, :],
                                      bg_wide[:, h0:h0 + 8, :].rearrange("p h n -> p (h n)"),
                                      start=True, stop=False, skip_group_check=True)
                            for j in range(4):
                                out = bank_g[X][:, :].rearrange("p (h n) -> p h n", h=8)
                                mm = pe.matmul(out[:, :, 16 * j:16 * j + 16], feats[:, par, 4 * X + j, :],
                                               wbox[:, h0:h0 + 8, :],
                                               start=False, stop=(j == 3), skip_group_check=True)
                        mm.then_inc(s_box, 1)

                def turn_probs(b, g):
                    t = G * b + g
                    pe.wait_ge(s_gated if boxes else s_exp, t + 1)
                    if not (isinstance(t, int) and t == 0):
                        pe.wait_ge(s_pT, t)
                    for i in range(HG):
                        mm = pe.transpose(bank_p[:, i * S:(i + 1) * S], probs[:, g, i, :],
                                          core.ident[:, :])
                    mm.then_inc(s_turn, 1)

                def weigh_values(b, par, g):
                    t = G * b + g
                    pe.wait_ge(s_pT, t + 1)
                    if rope:
                        if g == 0 and not (isinstance(b, int) and b == 0):
                            pe.wait_ge(s_raw, b)
                        if g == 0:
                            pe.wait_ge(s_val, b + 1)
                        pe.matmul(bank_o[32 * g:32 * g + 32, :], val[:, par, g, :],
                                  probsT[:, :, :].rearrange("p h n -> p (h n)"), start=True, stop=True)\
                            .then_inc(s_ctx, 1)
                        return
                    if not (isinstance(t, int) and t == 0):
                        pe.wait_ge(s_norm, t)
                    if g == 0 and not rope:
                        pe.wait_ge(s_mov[0], FILLS[0] * (b + 1))
                        pe.wait_ge(s_mov[1], FILLS[1] * (b + 1))
                    for i in range(HG):
                        mm = pe.matmul(bank_o[:, i * VW:(i + 1) * VW], probsT[:, i, :],
                                       val[:, par, head(g, i), :], start=True, stop=True)
                    mm.then_inc(s_ctx, 1)

                def turn_context(b, par, half, back):
                    pe.wait_ge(s_norm, G * b + 2 * half + 2)
                    cs = range(4 * half, 4 * half + 4)
                    if half == 0 and back >= 1:
                        pe.wait_ge(tail.res_step, tail_k * b - tail_k + 1)
                    if half == 1 and back >= 1:
                        tail.bank_free(pe, b - 1)
                    for c in cs:
                        mm = pe.transpose(bank_t[:, (c % 4) * S:(c % 4 + 1) * S],
                                          ctx[:, par, :, :].rearrange("p h d -> p (h d)")
                                          [:, c * 128:(c + 1) * 128], core.ident[:, :])
                    mm.then_inc(s_cT, 1)

                tail_k = 3 + (bias is not None)

                def turn_back(b):
                    pe.wait_ge(s_raw, b + 1)
                    if not (isinstance(b, int) and b == 0):
                        pe.wait_ge(s_cTm, b)
                    for i in range(HG):
                        mm = pe.transpose(bank_g[0][:, i * S:(i + 1) * S], raw[:, i, :], core.ident[:, :])
                    mm.then_inc(s_back, 1)

                def turn_context_whole(b, par):
                    pe.wait_ge(s_norm, b + 1)
                    pe.transpose(bank_g[0][:, 0:S], ctx[:, par, :, :].rearrange("p h d -> p (h d)"),
                                 core.ident[:, :]).then_inc(s_cT, 1)

                def batch_rope(b, par, back, more, here=True):
                    for g in range(G):
                        if here:
                            scores(b, par, g, back == 0)
                        if g == 0 and back == 2:
                            turn_context_whole(b - 2, par)
                        if g == 3 and here:
                            weigh_values(b, par, 0)
                        elif g < 3 and back:
                            weigh_values(b - 1, 1 - par, g + 1)
                        if g == 1 and back == 2:
                            project_out(b - 2)
                        if g >= 2 and here:
                            turn_probs(b, g - 2)
                        elif g < 2 and back:
                            turn_probs(b - 1, g + 2)
                        if more:
                            project(b + 1, 1 - par, g)
                        if g == 3 and back:
                            turn_back(b - 1)
                        if g == 3 and back == 2:
                            turn_x(b - 2, par, False)

                def drain_rope():
                    batch_rope(NB, 0, 2, False, False)
                    b, par = NB - 1, 1
                    turn_context_whole(b, par)
                    project_out(b)
                    turn_x(b, par, False)

                def project_out(b):
                    pe.wait_ge(s_cTm, HALVES * (b + 1))
                    for c in range(CH):
                        mm = pe.matmul(bank_t[:, 0:D], ctxT[:, c, :], wo[:, c, :], start=(c == 0),
                                       stop=(c == CH - 1))
                    mm.then_inc(tail.out_ready, 1)

                def turn_x(b, par, half0_next):
                    if half0_next:
                        pe.wait_ge(s_cTm, HALVES * (b + 1) + 1)
                    else:
                        pe.wait_ge(tail.res_step, tail_k * b + 1)
                    tail.turn_x(pe, b, par, bank_t)

                def batch(b, par, back, more, here=True):
                    for g in range(G):
                        if here:
                            scores(b, par, g, back == 0)
                        if more and boxes and g > 0:
                            project(b + 1, 1 - par, g - 1, (1,))
                        if g == 0 and back == 2:
                            project_out(b - 2)
                        if g == 3 and here:
                            weigh_values(b, par, 0)
                        elif g < 3 and back:
                            weigh_values(b - 1, 1 - par, g + 1)
                        if g == 3 and back == 2:
                            tail.route(pe, b - 2, bank_t)
                        if g >= 2 and here:
                            turn_probs(b, g - 2)
                        elif g < 2 and back:
                            turn_probs(b - 1, g + 2)
                        if more:
                            project(b + 1, 1 - par, g, (0,) if boxes else (0, 1))
                        if g == 1 and back and not rope:
                            turn_context(b - 1, 1 - par, 0, back - 1)
                        if g == 2 and back == 2:
                            turn_x(b - 2, par, not rope)
                        if g == 3 and back:
                            turn_context(b - 1, 1 - par, 1, back - 1)

                def drain():
                    batch(NB, 0, 2, False, False)
                    b, par = NB - 1, 1
                    project_out(b)
                    turn_x(b, par, False)
                    tail.route(pe, b, bank_t)

                pe.wait_ge(s_w, 16 * n_w)
                if not rope:
                    pe.wait_ge(core.att_loaded, 128 if boxes else 64)
                if boxes:
                    pe.wait_ge(s_bias, 1)
                    for c in range(CH):
                        mm = pe.matmul(bank_t[:, 0:D], bv_wide[:, c, :], wo[:, c, :], start=(c == 0),
                                       stop=(c == CH - 1))
                    mm.then_inc(s_bias, 1)
                    pe.wait_ge(s_bias, 3)
                    pe.wait_ge(s_bg, 10)
                for part in range(4):
                    project(0, 0, part)
                in_pairs(pe, *((batch_rope, drain_rope) if rope else (batch, drain)))

            @block.vector
            def _(v):
                v.wait_ge(s_w, 16 * n_w)
                if rope:
                    v.memset(val[:, :, :, hd + 1:VW], 0.0)
                v.memset(val[:, :, :, hd:hd + 1], 1.0).then_inc(s_ones, 1)
                if rope:
                    v.memset(qpad[:, :, :], 0.0).then_inc(s_ones, 1)
                    v.memset(kpad[:, :, :], 0.0).then_inc(s_ones, 1)
                    v.wait_ge(s_ones, 3)
                if boxes:
                    v.tensor_copy(bv_wide[:, :, :], bv[:, :].rearrange("p (c a) -> p c a", a=1)
                                  .broadcast_to([128, CH, 128])).then_inc(s_bias, 1)
                    v.wait_ge(s_bias, 2)
                    v.tensor_tensor(bias[:, :], bias[:, :], bank_t[:, 0:D], ALU.add).then_inc(s_bias, 1)
                    v.memset(ones[:, :], 1.0).then_inc(s_bg, 1)
                    v.memset(bg_wide[:, :, :], 0.0).then_inc(s_bg, 1)
                    n = 2
                    for part in range(3):
                        v.tensor_copy(bg_part[:, part, :], bg_rest[:, :]).then_inc(s_bg, 1)
                        n += 1
                        v.wait_ge(s_bg, n)
                        if part < 2:
                            v.tensor_tensor(bg_rest[:, :], bg_rest[:, :], bg_part[:, part, :], ALU.subtract)\
                                .then_inc(s_bg, 1)
                            n += 1
                            v.wait_ge(s_bg, n)
                    for part in range(3):
                        r = 32 * part
                        v.tensor_copy(bg_wide[r:r + 1, :, :],
                                      bg_part[r:r + 1, part, :].rearrange("p (h n) -> p h n", n=1)
                                      .broadcast_to([1, H, 64])).then_inc(s_bg, 1)

                def rotate(b, par):
                    v.wait_ge(s_prj[0], 2 * b + 1)
                    v.tensor_tensor(z[:, :], bank_j[0][:, 0:192], bqkv[:, :], ALU.add).then_inc(s_mov[0], 1)
                    v.wait_ge(s_mov[0], 2 * b + 1)
                    z3 = z[:, 0:160].rearrange("p (h d) -> p h d", d=8)
                    zc3 = zc[:, :].rearrange("p (h d) -> p h d", d=8)
                    zs3 = zs[:, :].rearrange("p (h d) -> p h d", d=8)

                    def wide(t, a, e):
                        return t[:, a:e].rearrange("p (a d) -> p a d", a=1).broadcast_to([128, 20, e - a])
                    v.tensor_tensor(zc3, z3, wide(cos, 0, 8), ALU.mult)
                    v.tensor_tensor(zs3[:, :, 0:4], z3[:, :, 1:8:2], wide(sin, 0, 4), ALU.mult)
                    v.tensor_tensor(zs3[:, :, 4:8], z3[:, :, 0:8:2], wide(sin, 4, 8), ALU.mult)\
                        .then_inc(s_rope, 1)
                    v.wait_ge(s_rope, b + 1)
                    def by_group(t3):
                        return t3.rearrange("p (g i) d -> p g i d", g=G)
                    v.tensor_tensor(qpad[:, :, 0:8].rearrange("p (i g) d -> p g i d", g=G),
                                    by_group(zc3[:, 0:16, :]), by_group(zs3[:, 0:16, :]), ALU.add)
                    v.tensor_tensor(kpad[:, :, 0:8], zc3[:, 16:20, :], zs3[:, 16:20, :], ALU.add)\
                        .then_inc(s_pad, 1)

                def empty(b, par, part):
                    if rope:
                        if part == 0:
                            rotate(b, par)
                        if part == 2:
                            v.wait_ge(s_prj[1], b + 1)
                            v.tensor_copy(val[:, par, :, 0:hd],
                                          z[:, 160:192].rearrange("p (h d) -> p h d", d=hd))\
                                .then_inc(s_val, 1)
                        return
                    if part == 3:
                        return
                    v.wait_ge(s_prj[1], 3 * b + part + 1)
                    dst = (qT, kT)[part][:, par, 4:8, :] if part < 2 else val[:, par, 8:16, 0:hd]
                    if boxes and part < 2:
                        bb = (bq, bk)[part][:, 4:8].rearrange("p (c a) -> p c a", a=1)\
                            .broadcast_to([128, 4, S])
                        v.tensor_tensor(dst, bank_j[1][:, :].rearrange("p (c n) -> p c n", c=4), bb, ALU.add)\
                            .then_inc(s_mov[1], 1)
                    elif part < 2:
                        v.tensor_copy(dst.rearrange("p c n -> p (c n)"), bank_j[1][:, :]).then_inc(s_mov[1], 1)
                    else:
                        v.tensor_copy(dst, bank_j[1][:, :].rearrange("p (h d) -> p h d", d=hd))\
                            .then_inc(s_mov[1], 1)

                def gate(b, g):
                    t = G * b + g
                    v.wait_ge(s_exp, t + 1)
                    if g % 2 == 0:
                        v.wait_ge(s_box, 2 * b + g // 2 + 1)
                    for X in range(2):
                        p = probs[:, g, :, 64 * X:64 * X + 64]
                        box = bank_g[X][:, :].rearrange("p (h n) -> p h n", h=8)[:, g % 2:8:2, :]
                        ins = v.scalar_tensor_tensor(out=p, in0=box, scalar=CLIP, in1=p,
                                                     op0=ALU.max, op1=ALU.mult)
                    ins.then_inc(s_gated, 1)

                def shift(b, g, first):
                    t = G * b + g
                    sc = bank_s[g % 2][:, :].rearrange("p (h n) -> p h n", h=HG)
                    v.wait_ge(s_scores, t + 1)
                    v.tensor_reduce(top[:, g % 2, :], sc, AX.X, ALU.max).then_inc(s_top, 1)
                    v.wait_ge(s_top, t + 1)
                    if not (first and g < 2):
                        v.wait_ge(s_exp, t - 1)
                    v.tensor_tensor(shifted[:, g % 2, :, :], sc,
                                    top[:, g % 2, :].rearrange("p (h a) -> p h a", a=1)
                                    .broadcast_to([128, HG, S]), ALU.subtract).then_inc(s_shift, 1)

                def scale_context(b, par, g):
                    t = G * b + g
                    o3 = bank_o[:, 0:HG * VW].rearrange("p (h d) -> p h d", d=VW)
                    v.wait_ge(s_ctx, t + 1)
                    v.reciprocal(inv[:, :].rearrange("p (h a) -> p h a", a=1), o3[:, :, hd:VW])\
                        .then_inc(s_inv, 1)
                    v.wait_ge(s_inv, t + 1)
                    h0 = head(g, 0)
                    v.tensor_tensor(ctx[:, par, h0:h0 + 7:2, :], o3[:, :, 0:hd],
                                    inv[:, :].rearrange("p (h a) -> p h a", a=1)
                                    .broadcast_to([128, HG, hd]), ALU.mult).then_inc(s_norm, 1)

                def scale_whole(b, par):
                    o4 = bank_g[0][:, :].rearrange("p (i g d) -> p g i d", i=HG, g=G)
                    i4 = inv_all[:, :].rearrange("p (g i a) -> p g i a", g=G, a=1)
                    v.wait_ge(s_back, b + 1)
                    v.reciprocal(i4, o4[:, :, :, hd:hd + 1]).then_inc(s_inv, 1)
                    v.wait_ge(s_inv, b + 1)
                    v.tensor_tensor(ctx[:, par, :, :].rearrange("p (g i) d -> p g i d", g=G),
                                    o4[:, :, :, 0:hd], i4.broadcast_to([128, G, HG, hd]), ALU.mult)\
                        .then_inc(s_norm, 1)

                def residual(b, par):
                    if rope and isinstance(b, int) and b == 0:
                        v.wait_ge(s_x, 16)
                    tail.residual(v, b, bank_t[:, 0:D], core.x_all[:, bass.ts(b, D)])

                def batch(b, par, back, more, here=True):
                    for g in range(G):
                        if g == 1 and back == 2:
                            residual(b - 2, par)
                        if here:
                            shift(b, g, back == 0)
                        if more and boxes and g > 0:
                            empty(b + 1, 1 - par, g - 1)
                        if g == 2 and back == 2:
                            tail.normalise(v, b - 2, par)
                        if g == 3 and back == 2:
                            tail.move_logits(v, b - 2)
                        if g == 3 and here:
                            scale_context(b, par, 0)
                        elif g < 3 and back:
                            scale_context(b - 1, 1 - par, g + 1)
                        if boxes and here:
                            gate(b, g)
                        if more and not boxes:
                            empty(b + 1, 1 - par, g)

                def drain():
                    batch(NB, 0, 2, False, False)
                    b, par = NB - 1, 1
                    residual(b, par)
                    tail.normalise(v, b, par)
                    tail.move_logits(v, b)

                def batch_rope(b, par, back, more, here=True):
                    for g in range(G):
                        if here:
                            shift(b, g, back == 0)
                        if g == 2 and back == 2:
                            residual(b - 2, par)
                        if g == 3 and back == 2:
                            tail.normalise(v, b - 2, par)
                        if more:
                            empty(b + 1, 1 - par, g)
                        if g == 3 and back:
                            scale_whole(b - 1, 1 - par)

                def drain_rope():
                    batch_rope(NB, 0, 2, False, False)
                    residual(NB - 1, 1)
                    tail.normalise(v, NB - 1, 1)

                for part in range(4):
                    empty(0, 0, part)
                in_pairs(v, *((batch_rope, drain_rope) if rope else (batch, drain)))

            @block.scalar
            def _(act):
                def empty(b, par, part):
                    if rope:
                        if part == 2:
                            act.wait_ge(s_prj[0], 2 * b + 2)
                            act.activation(kT[:, par, 0, :], bank_j[0][:, 0:S], ACT.Copy)\
                                .then_inc(s_mov[0], 1)
                            act.wait_ge(s_prj[1], b + 1)
                            act.activation(qT[:, par, :, :].rearrange("p c n -> p (c n)"), bank_j[1][:, :],
                                           ACT.Copy).then_inc(s_mov[1], 1)
                        return
                    if part == 3:
                        return
                    act.wait_ge(s_prj[0], 3 * b + part + 1)
                    if part == 2:
                        act.activation(val[:, par, 0:8, 0:hd],
                                       bank_j[0][:, :].rearrange("p (h d) -> p h d", d=hd), ACT.Copy)\
                            .then_inc(s_mov[0], 1)
                        return
                    dst = (qT, kT)[part]
                    if not boxes:
                        act.activation(dst[:, par, 0:4, :].rearrange("p c n -> p (c n)"), bank_j[0][:, :],
                                       ACT.Copy).then_inc(s_mov[0], 1)
                        return
                    for c in range(4):
                        ins = act.activation(dst[:, par, c, :], bank_j[0][:, c * S:(c + 1) * S], ACT.Identity,
                                             bias=(bq, bk)[part][:, c:c + 1])
                    ins.then_inc(s_mov[0], 1)

                def move_probs(b, g):
                    act.wait_ge(s_turn, G * b + g + 1)
                    act.activation(probsT[:, :, :].rearrange("p h n -> p (h n)"), bank_p[:, :], ACT.Copy)\
                        .then_inc(s_pT, 1)

                def exponentials(b, g, first):
                    t = G * b + g
                    act.wait_ge(s_shift, t + 1)
                    if not first:
                        act.wait_ge(s_turn, t - 3)
                    act.activation(probs[:, g, :, :].rearrange("p h n -> p (h n)"),
                                   shifted[:, g % 2, :, :].rearrange("p h n -> p (h n)"), ACT.Exp,
                                   scale=scale).then_inc(s_exp, 1)

                def move_context(b, half):
                    act.wait_ge(s_cT, HALVES * b + half + 1)
                    n = CH // HALVES
                    bank = bank_g[0] if rope else bank_t
                    act.activation(ctxT[:, n * half:n * half + n, :].rearrange("p c n -> p (c n)"),
                                   bank[:, 0:n * S], ACT.Copy).then_inc(s_cTm, 1)

                def move_raw(b):
                    act.wait_ge(s_ctx, G * b + G)
                    if not (isinstance(b, int) and b == 0):
                        act.wait_ge(s_back, b)
                    act.activation(raw[:, :, :].rearrange("p i n -> p (i n)"), bank_o[:, :], ACT.Copy)\
                        .then_inc(s_raw, 1)

                def batch(b, par, back, more, here=True):
                    for g in range(G):
                        if here and boxes:
                            exponentials(b, g, back == 0)
                        if g >= 2 and here:
                            move_probs(b, g - 2)
                        elif g < 2 and back:
                            move_probs(b - 1, g + 2)
                        if here and not boxes:
                            exponentials(b, g, back == 0)
                        if more:
                            empty(b + 1, 1 - par, g)
                        if g == 1 and back and not rope:
                            move_context(b - 1, 0)
                        if g == 2 and back == 2:
                            tail.move_xT(act, b - 2, bank_t)
                        if g == 3 and back:
                            move_context(b - 1, HALVES - 1)

                def drain():
                    batch(NB, 0, 2, False, False)
                    tail.move_xT(act, NB - 1, bank_t)

                def batch_rope(b, par, back, more, here=True):
                    for g in range(G):
                        if g == 0 and back == 2:
                            move_context(b - 2, 0)
                        if g == 2 and back:
                            move_raw(b - 1)
                        if g >= 2 and here:
                            move_probs(b, g - 2)
                        elif g < 2 and back:
                            move_probs(b - 1, g + 2)
                        if here:
                            exponentials(b, g, back == 0)
                        if more:
                            empty(b + 1, 1 - par, g)
                        if g == 3 and back == 2:
                            tail.move_xT(act, b - 2, bank_t)

                def drain_rope():
                    batch_rope(NB, 0, 2, False, False)
                    move_context(NB - 1, 0)
                    tail.move_xT(act, NB - 1, bank_t)

                for part in range(4):
                    empty(0, 0, part)
                in_pairs(act, *((batch_rope, drain_rope) if rope else (batch, drain)))

            @block.gpsimd
            def _(pool):
                pool_batches(pool, tail)


def pool_batches(pool, tail):
    tail.open_xT(pool)

    def batch(b, par):
        tail.rsqrt(pool, b)
        tail.keep(pool, b, par)
        tail.keep_T(pool, b)

    def pair(i):
        batch(2 * i, 0)
        batch(2 * i + 1, 1)
    first_apart(pool, NB // 2, pair)


def expert_phase(core, name, top2, out, emb=None):
    nc, dram = core.nc, core.dram
    st = ExitStack()
    with st:
        geo = Geometry(core, st, emb) if emb is not None else None
        sb = lambda n, shape, dt=F32: core.sb(f"{name}_{n}", shape, dt, stack=st)
        sem = lambda n: core.sem(f"{name}_{n}")
        w1h = sb("w1_high", [128, E, F], F32R)
        w1l = sb("w1_low", [128, E, F], F32R)
        xh = sb("x_high", [128, TB], F32R)
        xl = sb("x_low", [128, TB], F32R)
        w1, w2, hid = core.w1, core.w2, core.hid
        b1 = sb("b1", [128, E, FC])
        b2 = sb("b2", [E, D])
        order = sb("order", [128, E])
        acc = sb("acc", [128, TT, D])
        gates = sb("gates", [128, NB, E])
        gcur = sb("gcur", [128, TT, E])
        gT = sb("gT", [E, TB])
        t_a = sb("t_a", [128, NB, E])
        t_b = sb("t_b", [128, NB, E])
        m_a = sb("m_a", [128, NB])
        m_b = sb("m_b", [128, NB])
        m_c = sb("m_c", [128, NB])
        t_c = sb("t_c", [128, NB, E])
        stats = sb("stats", [128, TT, 6])
        mv = sb("mv", [128, TT, 2])
        vpe = sb("vpe", [128, TT])
        rstd = sb("rstd", [128, TT])
        bank_h = [core.ps(f"{name}_ps_h{k}", st) for k in range(FC)]
        bank_y = [core.ps(f"{name}_ps_y{k}", st) for k in range(2)]
        bank_g = core.ps(f"{name}_ps_gT", st)
        bank_b = core.ps(f"{name}_ps_bias", st)
        s_w = sem("weights_loaded")
        s_w1h = sem("w1_high_ready")
        s_w1l = sem("w1_low_ready")
        s_xh = sem("x_high_ready")
        s_xl = sem("x_low_ready")
        s_gs = sem("gate_step")
        s_gexp = sem("gate_exp")
        s_gcur = sem("gates_copied")
        s_gt = sem("gates_turned")
        s_gT = sem("gatesT_ready")
        s_b2 = sem("bias_ready")
        s_h = sem("hidden_ready")
        s_a = sem("activated")
        s_y = sem("y_ready")
        s_acc = sem("accumulated")
        s_ln = sem("norm_step")
        s_eps = sem("eps_added")
        s_rs = sem("rstd_ready")
        s_xn = sem("xn_ready")
        s_out = sem("stored")
        func = ACT.Relu if top2 else ACT.Gelu_apprx_tanh
        wp = "f1" if top2 else "f0"

        with nc.Block() as block:
            @block.sync
            def _(sp):
                sp.dma_start(b1[:, :, :].rearrange("p e c -> p (e c)"), dram[wp + "_b1"]).then_inc(s_w, 16)
                sp.dma_start(b2[:, :], dram[wp + "_b2"]).then_inc(s_w, 16)
                sp.dma_start(order[:, :], broadcast_rows(dram["order"], 128)).then_inc(s_w, 16)
                if geo:
                    geo.load(sp)
                    geo.store(sp)
                if out is not None:
                    with sp.Fori(0, NT) as i:
                        sp.wait_ge(s_xn, i + 1)
                        sp.dma_start(out[bass.ts(i, TT), :, :].rearrange("b p n -> p b n"),
                                     core.x_all[:, bass.ts(i, TB)].rearrange("p (b n) -> p b n", b=TT))\
                            .then_inc(s_out, 16)
                    sp.wait_ge(s_out, 16 * NT)

            @block.tensor
            def _(pe):
                def values(i, e):
                    pe.wait_ge(s_a, FC * E * i + FC * (e + 1))
                    if e >= 2 or not is_first(i):
                        pe.wait_ge(s_acc, E * i + e - 1)
                    for t in range(TT):
                        for c in range(FC):
                            mm = pe.matmul(bank_y[e % 2][:, t * D:(t + 1) * D],
                                           hid[:, e % 2, c, t * S:(t + 1) * S], w2[:, e, c, :],
                                           start=(c == 0), stop=(c == FC - 1))
                    mm.then_inc(s_y, 1)

                pe.wait_ge(s_w, 16 * 3)
                pe.wait_ge(core.experts_loaded, (2 if top2 else 1) * 32 * E)

                pe.wait_ge(s_w1l, E)

                def tokens(i):
                    pe.wait_ge(s_xl, i + 1)
                    for e in range(E):
                        for c in range(FC):
                            if e > 0 or not is_first(i):
                                pe.wait_ge(s_a, FC * E * i + FC * (e - 1) + c + 1)
                            cs = slice(c * 128, (c + 1) * 128)
                            pe.matmul(bank_h[c][:, :], w1h[:, e, cs], xh[:, :], start=True, stop=False)
                            pe.matmul(bank_h[c][:, :], w1l[:, e, cs], xh[:, :], start=False, stop=False)
                            pe.matmul(bank_h[c][:, :], w1h[:, e, cs], xl[:, :], start=False, stop=True)\
                                .then_inc(s_h, 1)
                        if e == 1:
                            pe.wait_ge(s_gcur, i + 1)
                            for t in range(TT):
                                mm = pe.transpose(bank_g[0:E, t * S:(t + 1) * S], gcur[:, t, :],
                                                  core.ident[:, :])
                            mm.then_inc(s_gt, 1)
                        if e == 2:
                            pe.wait_ge(s_gT, i + 1)
                            for t in range(TT):
                                mm = pe.matmul(bank_b[:, t * D:(t + 1) * D], gT[:, t * S:(t + 1) * S],
                                               b2[:, :], start=True, stop=True)
                            mm.then_inc(s_b2, 1)
                        if e > 0:
                            values(i, e - 1)
                    values(i, E - 1)
                first_apart(pe, NT, tokens)

            @block.scalar
            def _(act):
                act.wait_ge(s_w, 16 * 3)
                act.wait_ge(core.experts_loaded, (2 if top2 else 1) * 32 * E)

                def high(i):
                    act.activation(xh[:, :], core.xT_all[:, bass.ts(i, TB)], ACT.Copy).then_inc(s_xh, 1)
                for e in range(E):
                    act.activation(w1h[:, e, :], w1[:, e, :], ACT.Copy).then_inc(s_w1h, 1)
                high(0)
                if top2:
                    act.wait_ge(s_gs, 13)
                    act.activation(m_b[:, :], m_c[:, :], ACT.Exp).then_inc(s_gexp, 1)
                else:
                    act.wait_ge(s_gs, 6)
                    act.activation(t_b[:, :, :], t_a[:, :, :], ACT.Exp).then_inc(s_gexp, 1)
                act.wait_ge(s_w1l, E)

                def tokens(i):
                    for e in range(E):
                        for c in range(FC):
                            act.wait_ge(s_h, FC * (E * i + e) + c + 1)
                            act.activation(hid[:, e % 2, c, :], bank_h[c][:, :], func,
                                           bias=b1[:, e, c:c + 1]).then_inc(s_a, 1)
                        if e == E - 1 and not (isinstance(i, int) and i == NT - 1):
                            high(i + 1)
                        if geo:
                            geo.beside_act(act, i, e)
                first_apart(act, NT, tokens, 2 if geo else 1, 1)
                if geo:
                    geo.last_act(act)

            @block.vector
            def _(v):
                n = 0

                def did(ins):
                    nonlocal n
                    n += 1
                    ins.then_inc(s_gs, 1)
                    v.wait_ge(s_gs, n)

                v.wait_ge(s_w, 16 * 3)
                v.wait_ge(core.experts_loaded, (2 if top2 else 1) * 32 * E)

                def low(i):
                    v.wait_ge(s_xh, i + 1)
                    v.tensor_tensor(xl[:, :], core.xT_all[:, bass.ts(i, TB)], xh[:, :].bitcast(F32),
                                    ALU.subtract).then_inc(s_xl, 1)
                for e in range(E):
                    v.wait_ge(s_w1h, e + 1)
                    v.tensor_tensor(w1l[:, e, :], w1[:, e, :], w1h[:, e, :].bitcast(F32), ALU.subtract)\
                        .then_inc(s_w1l, 1)
                low(0)
                lg = core.logits_all[:, :].rearrange("p (b e) -> p b e", e=E)

                def wide(t):
                    return t[:, :].rearrange("p (b a) -> p b a", a=1).broadcast_to([128, NB, E])
                rank = order[:, :].rearrange("p (a e) -> p a e", a=1).broadcast_to([128, NB, E])

                def first_of_largest(src_, top, pick, tmp, mt):
                    did(v.tensor_reduce(top[:, :], src_, AX.X, ALU.max))
                    did(v.tensor_tensor(pick[:, :, :], src_, wide(top), ALU.is_equal))
                    did(v.tensor_tensor(tmp[:, :, :], pick[:, :, :], rank, ALU.mult))
                    did(v.tensor_reduce(mt[:, :], tmp[:, :, :], AX.X, ALU.max))
                    did(v.tensor_tensor(pick[:, :, :], tmp[:, :, :], wide(mt), ALU.is_equal))

                first_of_largest(lg, m_a, gates, t_a, m_b)
                if not top2:
                    did(v.tensor_tensor(t_a[:, :, :], lg, wide(m_a), ALU.subtract))
                    v.wait_ge(s_gexp, 1)
                    did(v.tensor_reduce(m_b[:, :], t_b[:, :, :], AX.X, ALU.add))
                    did(v.reciprocal(m_b[:, :], m_b[:, :]))
                    did(v.tensor_tensor(gates[:, :, :], gates[:, :, :], wide(m_b), ALU.mult))
                else:
                    did(v.tensor_scalar(t_a[:, :, :], gates[:, :, :], NEG, None, ALU.mult))
                    did(v.tensor_tensor(t_b[:, :, :], t_a[:, :, :], lg, ALU.add))
                    first_of_largest(t_b[:, :, :], m_c, t_c, t_a, m_b)
                    did(v.tensor_tensor(m_c[:, :], m_c[:, :], m_a[:, :], ALU.subtract))
                    v.wait_ge(s_gexp, 1)
                    did(v.tensor_scalar(m_a[:, :], m_b[:, :], 1.0, None, ALU.add))
                    did(v.reciprocal(m_a[:, :], m_a[:, :]))
                    did(v.tensor_tensor(m_b[:, :], m_b[:, :], m_a[:, :], ALU.mult))
                    did(v.tensor_tensor(gates[:, :, :], gates[:, :, :], wide(m_a), ALU.mult))
                    did(v.tensor_tensor(t_c[:, :, :], t_c[:, :, :], wide(m_b), ALU.mult))
                    did(v.tensor_tensor(gates[:, :, :], gates[:, :, :], t_c[:, :, :], ALU.add))

                def tokens(i):
                    if not is_first(i):
                        v.wait_ge(s_gt, i)
                    v.tensor_copy(gcur[:, :, :].rearrange("p t e -> p (t e)"),
                                  gates[:, :, :].rearrange("p b e -> p (b e)")[:, bass.ts(i, TT * E)])\
                        .then_inc(s_gcur, 1)
                    v.wait_ge(s_gt, i + 1)
                    v.tensor_copy(gT[:, :], bank_g[0:E, :]).then_inc(s_gT, 1)
                    v.wait_ge(s_b2, i + 1)
                    v.tensor_tensor(acc[:, :, :].rearrange("p t d -> p (t d)"), bank_b[:, :],
                                    core.x_all[:, bass.ts(i, TB)], ALU.add).then_inc(s_ln, 1)
                    v.wait_ge(s_ln, 3 * i + 1)
                    for e in range(E):
                        v.wait_ge(s_y, E * i + e + 1)
                        if e > 0:
                            v.wait_ge(s_acc, E * i + e)
                        for t in range(TT):
                            ins = v.scalar_tensor_tensor(
                                out=acc[:, t, :], in0=bank_y[e % 2][:, t * D:(t + 1) * D],
                                scalar=gcur[:, t, e:e + 1], in1=acc[:, t, :], op0=ALU.mult, op1=ALU.add)
                        ins.then_inc(s_acc, 1)
                        if e == E - 2 and not (isinstance(i, int) and i == NT - 1):
                            low(i + 1)
                        if geo:
                            geo.beside_dve(v, i, e)
                    v.wait_ge(s_acc, E * i + E)
                    for t in range(TT):
                        ins = v.bn_stats(stats[:, t, :], acc[:, t, :])
                    ins.then_inc(s_ln, 1)
                    core.wait_apart(v, s_ln, 3 * i + 2)
                    for t in range(TT):
                        ins = v.bn_aggr(mv[:, t, :], stats[:, t, :])
                    ins.then_inc(s_ln, 1)
                    v.wait_ge(s_rs, i + 1)
                    for t in range(TT):
                        ins = v.tensor_scalar(core.x_all[:, bass.ds(i * TB + t * D, D)], acc[:, t, :],
                                              mv[:, t, 0:1], rstd[:, t:t + 1], ALU.subtract, ALU.mult)
                    ins.then_inc(s_xn, 1)
                first_apart(v, NT, tokens, 1, 1)
                if geo:
                    geo.reduce(v, NT - 1)

            @block.gpsimd
            def _(pool):
                with pool.Fori(0, NT) as i:
                    pool.wait_ge(s_ln, 3 * i + 3)
                    pool.tensor_tensor(vpe[:, :], mv[:, :, 1], core.eps_tile[:, :], ALU.add).then_inc(s_eps, 1)
                    pool.wait_ge(s_eps, i + 1)
                    pool.tensor_tensor(rstd[:, :], vpe[:, :], core.half_power[:, :], ALU.pow).then_inc(s_rs, 1)


def block_attention_phase(core, ahead):
    nc, dram = core.nc, core.dram
    name, HD, CH = "l1a", 64, 8
    QX, KX = 64, 96
    QW, KW = QX + S, S + KX
    VW = HD + 4
    FILLS = 10
    TAIL_STEPS = 4
    st = ExitStack()
    with st:
        sb = lambda n, shape, dt=F32: core.sb(f"{name}_{n}", shape, dt, stack=st)
        sem = lambda n: core.sem(f"{name}_{n}")
        bank_s = [core.ps(f"{name}_ps_scores{k}", st) for k in range(2)]
        bank_j = [core.ps(f"{name}_ps_project{k}", st) for k in range(2)]
        bank_o = [core.ps(f"{name}_ps_context{k}", st) for k in range(2)]
        bank_t = core.ps(f"{name}_ps_tail", st)
        bank_x = core.ps(f"{name}_ps_x", st)
        wq = sb("wq", [128, H * HD])
        wk = sb("wk", [128, H * HD])
        wv = sb("wv", [128, H * HD])
        wo = sb("wo", [128, CH, D])
        bias = sb("bias", [128, D])
        mask = sb("mask", [128, 2, 32])
        quad = sb("quad", [128, 4])
        level_w = sb("level_w", [128, 4])
        xs = sb("xs", [128, D])
        xe = sb("xe", [128, 2, QX + S + KX])
        pairs = sb("pairs", [128, 64])
        quads = sb("quads", [128, 32])
        qT = sb("qT", [128, 2, CH, QW])
        kT = sb("kT", [128, 2, CH, KW])
        val = sb("val", [128, 2, H, VW])
        shifted = sb("shifted", [128, 2, 16, 32])
        top = sb("top", [128, 2, 16])
        probs = sb("probs", [128, 2, 16, 32])
        fine = sb("fine", [128, 2, 8, 32])
        fineT = sb("fineT", [128, 2, 8, 32])
        probsT = sb("probsT", [128, 2, 8, S])
        sums = sb("sums", [128, HG, 4])
        inv = sb("inv", [128, HG])
        ctx = sb("ctx", [128, 2, H, HD])
        ctxT = sb("ctxT", [128, CH, S])
        tail = Tail(core, st, name, bias[:, :])
        tail.bank = bank_x
        s_w = sem("weights_loaded")
        s_set = sem("constants_set")
        s_xs = sem("x_copied")
        s_in = sem("x_in_turned")
        s_xe = sem("x_in_moved")
        s_pool = sem("pool_step")
        s_prj = [sem("projected0"), sem("projected1")]
        s_mov = [sem("moved0"), sem("moved1")]
        s_scores = sem("scores_ready")
        s_sh = sem("shift_step")
        s_shift = sem("shifted")
        s_exp = sem("exp_ready")
        s_fine = sem("expanded")
        s_fineT = sem("expanded_turned")
        s_placed = sem("far_placed")
        s_near = sem("near_placed")
        s_ctx = sem("context_ready")
        s_sum = sem("sum_step")
        s_norm = sem("context_scaled")
        s_cT = sem("context_turned")
        s_cTm = sem("contextT_ready")
        wl = [(wq[:, :], dram["a1_wq"]), (wk[:, :], dram["a1_wk"]), (wv[:, :], dram["a1_wv"]),
              (wo[:, :, :], dram["a1_wo"].rearrange("(c p) n -> p c n", p=128)),
              (bias[:, :], broadcast_rows(dram["a1_bo"], 128)),
              (mask[:, :, :].rearrange("p a n -> p (a n)"), dram["level_mask"]),
              (quad[:, :], dram["quadrant"]), (level_w[:, :], dram["level_weight"])]

        def heads(g):
            return [8 * (g // 2) + 2 * i + g % 2 for i in range(HG)]

        def empty_bank(copy, par, f):
            bank = bank_j[f % 2]
            if f < 8:
                t, n = (qT, QW) if f < 4 else (kT, KW)
                c = 2 * (f % 4)
                return copy(t[:, par, c:c + 2, :].rearrange("p c n -> p (c n)"), bank[:, 0:2 * n])
            h0 = 8 * (f - 8)
            return copy(val[:, par, h0:h0 + 8, 0:HD], bank[:, :].rearrange("p (h d) -> p h d", d=HD))

        with nc.Block() as block:
            @block.sync
            def _(sp):
                for t, source in wl:
                    sp.dma_start(t, source).then_inc(s_w, 16)
                ahead(sp)

            @block.tensor
            def _(pe):
                def turn_in(b):
                    pe.wait_ge(s_xs, b + 1)
                    pe.transpose(bank_x[:, 0:S], xs[:, :], core.ident[:, :]).then_inc(s_in, 1)

                def scores(b, par, X):
                    r = 64 * X
                    for c in range(CH):
                        for j in range(4):
                            p = 32 * j
                            pe.matmul(bank_s[X][p:p + 32, 32 * c:32 * c + 32],
                                      qT[r:r + 64, par, c, QX + p:QX + p + 32],
                                      kT[r:r + 64, par, c, p:p + 32], start=True, stop=True)
                        for j in range(3):
                            p = 32 * j
                            q0 = 32 if j == 2 else 0
                            k0 = S + 32 * j
                            mm = pe.matmul(bank_s[X][p:p + 32, 256 + 32 * c:288 + 32 * c],
                                           qT[r:r + 64, par, c, q0:q0 + 32],
                                           kT[r:r + 64, par, c, k0:k0 + 32], start=True, stop=True)
                    mm.then_inc(s_scores, 1)

                def project(b, par, *fills):
                    if 0 in fills:
                        pe.wait_ge(s_pool, 4 * (b + 1))
                    for f in fills:
                        k = f % 2
                        if not (isinstance(b, int) and b == 0 and f < 2):
                            pe.wait_ge(s_mov[k], 5 * b + f // 2)
                        if f < 8:
                            w, n, a = (wq, QW, 0) if f < 4 else (wk, KW, QX)
                            for cc in range(2):
                                c = 2 * (f % 4) + cc
                                mm = pe.matmul(bank_j[k][:, cc * n:(cc + 1) * n], w[:, c * 128:(c + 1) * 128],
                                               xe[:, par, a:a + n], start=True, stop=True)
                        else:
                            mm = pe.matmul(bank_j[k][:, :], xe[:, par, QX:QX + S],
                                           wv[:, (f - 8) * 512:(f - 7) * 512], start=True, stop=True)
                        mm.then_inc(s_prj[k], 1)

                def weigh_values(b, par, g):
                    X = g % 2
                    pe.wait_ge(s_near, 2 * b + X + 1)
                    pe.wait_ge(s_placed, 2 * b + X + 1)
                    if not (isinstance(b, int) and b == 0 and g < 2):
                        pe.wait_ge(s_norm, G * b + g - 1)
                    for i, h in enumerate(heads(g)):
                        mm = pe.matmul(bank_o[X][:, i * VW:(i + 1) * VW], probsT[:, X, h // 2, :],
                                       val[:, par, h, :], start=True, stop=True)
                    mm.then_inc(s_ctx, 1)

                def turn_context(b, par, half, wait):
                    pe.wait_ge(s_norm, G * b + 2 * half + 2)
                    if half == 0 and wait:
                        pe.wait_ge(tail.res_step, TAIL_STEPS * b - TAIL_STEPS + 1)
                    if half == 1:
                        pe.wait_ge(s_cTm, 2 * b + 1)
                    for c in range(4 * half, 4 * half + 4):
                        mm = pe.transpose(bank_t[:, (c % 4) * S:(c % 4 + 1) * S],
                                          ctx[:, par, :, :].rearrange("p h d -> p (h d)")
                                          [:, c * 128:(c + 1) * 128], core.ident[:, :])
                    mm.then_inc(s_cT, 1)

                def project_out(b):
                    pe.wait_ge(s_cTm, 2 * (b + 1))
                    for c in range(CH):
                        mm = pe.matmul(bank_t[:, 0:D], ctxT[:, c, :], wo[:, c, :], start=(c == 0),
                                       stop=(c == CH - 1))
                    mm.then_inc(tail.out_ready, 1)

                def batch(b, par, back, more):
                    ahead = not (isinstance(b, int) and b >= NB - 2)
                    for k in range(2):
                        pe.wait_ge(s_mov[k], 5 * b + 4)
                    if ahead:
                        turn_in(b + 2)
                    scores(b, par, 0)
                    scores(b, par, 1)
                    if more:
                        project(b + 1, 1 - par, 0, 1)
                    if back:
                        turn_context(b - 1, 1 - par, 1, True)
                    if more:
                        project(b + 1, 1 - par, 2, 3)
                    if back == 2:
                        if ahead:
                            pe.wait_ge(s_xe, b + 3)
                        tail.turn_x(pe, b - 2, par, bank_x)
                    if more:
                        project(b + 1, 1 - par, 4)
                    if back:
                        project_out(b - 1)
                    if more:
                        project(b + 1, 1 - par, 5, 6, 7)
                    for k in range(2):
                        pe.wait_ge(s_mov[k], 5 * (b + 1))
                    for g in range(G):
                        weigh_values(b, par, g)
                        if more and g < 2:
                            project(b + 1, 1 - par, 8 + g)
                    turn_context(b, par, 0, back > 0)

                def drain():
                    b = NB - 1
                    pe.wait_ge(tail.x_moved, b - 1)
                    tail.turn_x(pe, b - 1, 0, bank_x)
                    turn_context(b, 1, 1, True)
                    project_out(b)
                    pe.wait_ge(tail.x_moved, b)
                    tail.turn_x(pe, b, 1, bank_x)

                pe.wait_ge(s_w, 16 * len(wl))
                pe.wait_ge(s_set, 6)
                turn_in(0)
                pe.wait_ge(s_xe, 1)
                turn_in(1)
                project(0, 0, *range(FILLS))
                in_pairs(pe, batch, drain)

            @block.scalar
            def _(act):
                def move_in(b, par):
                    act.wait_ge(s_in, b + 1)
                    act.activation(xe[:, par, QX:QX + S], bank_x[:, 0:S], ACT.Copy).then_inc(s_xe, 1)

                def exponentials(b, X):
                    act.wait_ge(s_shift, 2 * b + X + 1)
                    act.activation(probs[:, X, :, :].rearrange("p h n -> p (h n)"),
                                   shifted[:, X, :, :].rearrange("p h n -> p (h n)"), ACT.Exp,
                                   scale=float(HD) ** -0.5).then_inc(s_exp, 1)

                def empty(b, par, fills):
                    for f in fills:
                        act.wait_ge(s_prj[f % 2], 5 * b + f // 2 + 1)
                        empty_bank(lambda o, i: act.activation(o, i, ACT.Copy), par, f)\
                            .then_inc(s_mov[f % 2], 1)

                def move_context(b, half):
                    act.wait_ge(s_cT, 2 * b + half + 1)
                    act.activation(ctxT[:, 4 * half:4 * half + 4, :].rearrange("p c n -> p (c n)"),
                                   bank_t[:, :], ACT.Copy).then_inc(s_cTm, 1)

                def batch(b, par, back, more):
                    def others(*fills):
                        if more:
                            empty(b + 1, 1 - par, fills)
                    if not (isinstance(b, int) and b >= NB - 2):
                        move_in(b + 2, par)
                    others(0)
                    exponentials(b, 0)
                    others(1)
                    if back:
                        move_context(b - 1, 1)
                    others(2)
                    exponentials(b, 1)
                    others(3)
                    if back == 2:
                        tail.move_xT(act, b - 2, bank_x)
                    others(4, 5, 6, 7, 8, 9)
                    move_context(b, 0)

                def drain():
                    b = NB - 1
                    tail.move_xT(act, b - 1, bank_x)
                    move_context(b, 1)
                    tail.move_xT(act, b, bank_x)

                act.wait_ge(s_set, 6)
                move_in(0, 0)
                move_in(1, 1)
                empty(0, 0, range(FILLS))
                in_pairs(act, batch, drain)

            @block.vector
            def _(v):
                def shift(b, X):
                    n = 2 * b + X
                    sc = shifted[:, X, :, :].rearrange("p (l h) n -> p l h n", l=2)
                    v.wait_ge(s_scores, n + 1)
                    v.tensor_tensor(sc, bank_s[X][:, :].rearrange("p (l h n) -> p l h n", l=2, h=8),
                                    mask[:, :, :].rearrange("p l (h n) -> p l h n", h=1)
                                    .broadcast_to([128, 2, 8, 32]), ALU.add).then_inc(s_sh, 1)
                    v.wait_ge(s_sh, 2 * n + 1)
                    v.tensor_reduce(top[:, X, :], shifted[:, X, :, :], AX.X, ALU.max).then_inc(s_sh, 1)
                    v.wait_ge(s_sh, 2 * n + 2)
                    v.tensor_tensor(shifted[:, X, :, :], shifted[:, X, :, :],
                                    top[:, X, :].rearrange("p (h a) -> p h a", a=1)
                                    .broadcast_to([128, 16, 32]), ALU.subtract).then_inc(s_shift, 1)

                def spread(b, X):
                    n = 2 * b + X
                    v.wait_ge(s_exp, n + 1)
                    near = probs[0:96, X, 8:16, 0:16].rearrange("p h (m a) -> p h m a", a=1)
                    v.tensor_copy(fine[0:96, X, :, :].rearrange("p h (m a) -> p h m a", a=2),
                                  near.broadcast_to([96, 8, 16, 2])).then_inc(s_fine, 1)
                    for j in range(4):
                        p = 32 * j
                        v.transpose(probsT[p:p + 32, X, :, p:p + 32], probs[p:p + 32, X, 0:8, :])
                    v.wait_ge(s_fine, 2 * n + 1)
                    far = probs[0:96, X, 8:16, 16:24].rearrange("p h (m a) -> p h m a", a=1)
                    f4 = fine[0:96, X, :, :].rearrange("p h (m a) -> p h m a", a=4)
                    v.tensor_tensor(f4, f4, far.broadcast_to([96, 8, 8, 4]), ALU.add).then_inc(s_fine, 1)
                    v.wait_ge(s_fine, 2 * n + 2)
                    v.transpose(fineT[0:96, X, :, :], fine[0:96, X, :, :]).then_inc(s_fineT, 1)
                    v.wait_ge(s_fineT, n + 1)
                    v.tensor_copy(probsT[64:96, X, :, 97:128:2], fineT[64:96, X, :, 0:16])\
                        .then_inc(s_near, 1)

                def scale_context(b, par, g):
                    t = G * b + g
                    o3 = bank_o[g % 2][:, 0:HG * VW].rearrange("p (h d) -> p h d", d=VW)
                    v.wait_ge(s_ctx, t + 1)
                    v.tensor_tensor(sums[:, :, :], o3[:, :, HD:VW],
                                    level_w[:, :].rearrange("p (a q) -> p a q", a=1)
                                    .broadcast_to([128, HG, 4]), ALU.mult).then_inc(s_sum, 1)
                    v.wait_ge(s_sum, 4 * t + 1)
                    v.tensor_reduce(inv[:, :], sums[:, :, :], AX.X, ALU.add).then_inc(s_sum, 1)
                    v.wait_ge(s_sum, 4 * t + 2)
                    v.tensor_scalar(inv[:, :], inv[:, :], 1e-8, None, ALU.add).then_inc(s_sum, 1)
                    v.wait_ge(s_sum, 4 * t + 3)
                    v.reciprocal(inv[:, :], inv[:, :]).then_inc(s_sum, 1)
                    v.wait_ge(s_sum, 4 * t + 4)
                    h0 = heads(g)[0]
                    v.tensor_tensor(ctx[:, par, h0:h0 + 7:2, :], o3[:, :, 0:HD],
                                    inv[:, :].rearrange("p (h a) -> p h a", a=1)
                                    .broadcast_to([128, HG, HD]), ALU.mult).then_inc(s_norm, 1)

                def batch(b, par, back, more):
                    shift(b, 0)
                    if back == 2:
                        tail.normalise(v, b - 2, par)
                    shift(b, 1)
                    spread(b, 0)
                    spread(b, 1)
                    if back:
                        tail.residual(v, b - 1, bank_t[:, 0:D], core.x_all[:, bass.ts(b - 1, D)])
                    for g in range(G):
                        scale_context(b, par, g)

                def drain():
                    b = NB - 1
                    tail.normalise(v, b - 1, 0)
                    tail.residual(v, b, bank_t[:, 0:D], core.x_all[:, bass.ts(b, D)])
                    tail.normalise(v, b, 1)

                v.wait_ge(s_w, 16 * len(wl))
                v.memset(probsT[:, :, :, :], 0.0).then_inc(s_set, 1)
                for X in range(2):
                    v.memset(bank_s[X][96:128, 256:512], 0.0).then_inc(s_set, 1)
                for par in range(2):
                    v.tensor_copy(val[:, par, :, HD:VW], quad[:, :].rearrange("p (a q) -> p a q", a=1)
                                  .broadcast_to([128, H, 4])).then_inc(s_set, 1)
                v.memset(fine[:, :, :, :], 0.0).then_inc(s_set, 1)
                v.wait_ge(s_set, 6)
                in_pairs(v, batch, drain)

            @block.gpsimd
            def _(pool):
                def copy_in(b):
                    pool.tensor_copy(xs[:, :], core.x_all[:, bass.ts(b, D)]).then_inc(s_xs, 1)

                def half(n):
                    return core.half[:, :].broadcast_to([128, n])

                def pool_x(b, par):
                    x = xe[:, par, QX:QX + S]
                    pool.wait_ge(s_xe, b + 1)
                    pool.tensor_tensor(pairs[:, :], x[:, 0:S:2], x[:, 1:S:2], ALU.add).then_inc(s_pool, 1)
                    pool.wait_ge(s_pool, 4 * b + 1)
                    pool.tensor_tensor(pairs[:, :], pairs[:, :], half(64), ALU.mult).then_inc(s_pool, 1)
                    pool.wait_ge(s_pool, 4 * b + 2)
                    pool.tensor_tensor(quads[:, :], pairs[:, 0:64:2], pairs[:, 1:64:2], ALU.add)\
                        .then_inc(s_pool, 1)
                    pool.wait_ge(s_pool, 4 * b + 3)
                    k0 = QX + S
                    for a, q0, n in ((16, 16, 16), (48, 16, 16), (k0 + 16, 0, 16), (k0 + 48, 8, 8),
                                     (k0 + 56, 0, 8), (k0 + 80, 0, 16)):
                        pool.tensor_tensor(xe[:, par, a:a + n], quads[:, q0:q0 + n], half(n), ALU.mult)
                    for a, p0 in ((0, 16), (32, 48), (k0, 0), (k0 + 32, 0), (k0 + 64, 32)):
                        ins = pool.tensor_copy(xe[:, par, a:a + 16], pairs[:, p0:p0 + 16])
                    ins.then_inc(s_pool, 1)

                def place(b, X):
                    pool.wait_ge(s_fineT, 2 * b + X + 1)
                    pool.tensor_tensor(probsT[0:32, X, :, 33:64:2], fineT[0:32, X, :, 0:16],
                                       core.zeros[0:32, :].rearrange("p (a n) -> p a n", a=1)
                                       .broadcast_to([32, 8, 16]), ALU.add)
                    pool.tensor_copy(probsT[0:64, X, :, 67:128:4], fineT[0:64, X, :, 16:32])\
                        .then_inc(s_placed, 1)

                def batch(b, par, back, more):
                    if not (isinstance(b, int) and b >= NB - 2):
                        copy_in(b + 2)
                        pool_x(b + 2, par)
                    if back == 2:
                        tail.keep(pool, b - 2, par)
                        tail.keep_T(pool, b - 2)
                    place(b, 0)
                    place(b, 1)
                    if back:
                        tail.rsqrt(pool, b - 1)

                def drain():
                    b = NB - 1
                    tail.keep(pool, b - 1, 0)
                    tail.keep_T(pool, b - 1)
                    tail.rsqrt(pool, b)
                    tail.keep(pool, b, 1)
                    tail.keep_T(pool, b)

                tail.open_xT(pool)
                copy_in(0)
                pool_x(0, 0)
                copy_in(1)
                pool_x(1, 1)
                in_pairs(pool, batch, drain)


def decoder_kernel(nc, dram, out, emb):
    stack = ExitStack()
    with stack:
        core = Core(nc, stack, dram)
        setup_phase(core)
        core.end_phase()
        attention_phase(core, "l0a", "rope", 8, float(8) ** -0.5, True, None, "a0",
                        lambda sp: core.load_attention(sp, "x0"))
        core.end_phase()
        attention_phase(core, "l0x", "cross", 64, float(64) ** -0.5, False, "f0_router", "x0",
                        lambda sp: core.load_experts(sp, "f0"))
        core.end_phase()
        expert_phase(core, "l0f", False, None, emb)
        core.end_phase()
        block_attention_phase(core, lambda sp: core.load_attention(sp, "x1"))
        core.end_phase()
        attention_phase(core, "l1x", "boxes", 64, float(64) ** -0.5, True, "f1_router", "x1",
                        lambda sp: core.load_experts(sp, "f1"), emb)
        core.end_phase()
        expert_phase(core, "l1f", True, out)


def constants():
    f = np.float32
    c = {"identity": np.eye(128, dtype=f)}
    inv_freq = (f(1.0) / f(10000.0) ** (np.arange(0, 8, 2, dtype=f) / f(8))).astype(f)
    ang = (np.arange(S, dtype=f)[:, None] * inv_freq[None, :]).astype(f)
    cos, sin = np.cos(ang).astype(f), np.sin(ang).astype(f)
    c["rope_cos"] = np.concatenate([cos, cos], 1)
    c["rope_sin"] = np.concatenate([-sin, sin], 1)
    c["order"] = np.arange(E, 0, -1).astype(f)
    r = np.arange(32)
    near = (r[:, None] // 16 == r[None, :] // 16) & (r[None, :] <= r[:, None])
    far = r[:, None] // 16 == r[None, :] // 16
    m = np.where(np.concatenate([near, far], 1), 0.0, NEG).astype(f)
    c["level_mask"] = np.tile(m, (4, 1))
    q = np.arange(128) // 32
    c["quadrant"] = (q[:, None] == np.arange(4)[None, :]).astype(f)
    lw = np.array([[1, 0, 0, 0], [.5, 1, 0, 0], [.25, .25, 1, 0], [.25, .25, .5, 1]], dtype=f)
    c["level_weight"] = lw[q]
    return c


def host_arrays(x, ctx_1024, fside_BxSx4_0, **w):
    a = {k: np.asarray(v) for k, v in w.items()}
    x, ctx, box = np.asarray(x), np.asarray(ctx_1024), np.asarray(fside_BxSx4_0)
    c = {"x": x, "xT": x.transpose(0, 2, 1), "ctxT": ctx.transpose(0, 2, 1)}
    boxT = box.transpose(0, 2, 1)
    c["boxesT"] = boxT
    for side, key in ((0, "boxes_lo_j"), (1, "boxes_hi_j")):
        t = boxT[:, 2 * side:2 * side + 2, :].reshape(NB // 2, 2, 2, 8, 16)
        t = t.transpose(1, 2, 4, 0, 3).reshape(64, NB // 2 * 8)
        c[key] = np.concatenate([t, t], 0)
    c["a0_wqkv"] = np.concatenate([a["L0_attn_Wq"].T, a["L0_attn_Wk"].T, a["L0_attn_Wv"].T], 1)
    c["a0_bqkv"] = np.concatenate([a["L0_attn_bq"], a["L0_attn_bk"], a["L0_attn_bv"]])
    c["a0_wo"] = a["L0_attn_Wo"].T
    c["a0_bo"] = a["L0_attn_bo"]
    for k in ("q", "k", "v", "o"):
        c["x0_w" + k] = a["L0_xattn_W" + k]
        c["x1_w" + k] = a["L1_xattn_W" + k].T
    qkv = a["L1_attn_w_qkv"]
    for i, k in enumerate("qkv"):
        c["a1_w" + k] = qkv[i * 1024:(i + 1) * 1024].T
    c["a1_wo"] = a["L1_attn_w_out"].T
    c["a1_bo"] = a["L1_attn_b_out"]
    for k in ("q", "k", "v"):
        c["x1_b" + k] = a["L1_xattn_b" + k].reshape(8, 128).T
    c["x1_bo"] = a["L1_xattn_bo"]
    c["x1_bg"] = a["L1_xattn_bg"]
    wg = a["L1_xattn_Wg"]
    sel = np.zeros((8, 16, H, 16), np.float32)
    for j in range(16):
        sel[:, j, :, j] = wg.T
    c["x1_wbox_sel"] = sel.reshape(128, H * 16)
    for p, n in (("f0", "L0_ffn_"), ("f1", "L1_ffn_")):
        r = "switch_" if p == "f0" else "router_"
        c[p + "_router_w"], c[p + "_router_b"] = a[n + r + "w"], a[n + r + "b"]
        c[p + "_w1"], c[p + "_w2"], c[p + "_b2"] = a[n + "w1"], a[n + "w2"], a[n + "b2"]
        c[p + "_b1"] = a[n + "b1"].reshape(E, FC, 128).transpose(2, 0, 1).reshape(128, E * FC)
    c.update(constants())
    return {k: np.ascontiguousarray(v) for k, v in c.items()}


def kernel(**inputs):
    import concourse.bacc as bacc
    from concourse.bass_utils import run_bass_kernel_spmd

    nc = bacc.Bacc("TRN2", target_bir_lowering=False, num_devices=1)
    arrays = {"in_" + k: v for k, v in host_arrays(**inputs).items()}
    dram = {k[3:]: nc.dram_tensor(k, v.shape, mybir.dt.from_np(v.dtype), kind="ExternalInput").ap()
            for k, v in arrays.items()}
    out = nc.dram_tensor("out_x", (NB, S, D), F32, kind="ExternalOutput").ap()
    emb = nc.dram_tensor("box_features", (NB // 2, 2, 128, 8 * S), F32, kind="Internal").ap()
    decoder_kernel(nc, dram, out, emb)
    r = run_bass_kernel_spmd(nc, [arrays], core_ids=[0])
    return r.results[0]["out_x"]
```
